# Optimizing a Trainium2 kernel written in Bass

```python
import numpy as np
import jax
import jax.numpy as jnp

def _softmax(x, axis=-1):
    return jax.nn.softmax(x, axis=axis)

def _gelu(x):
    return jax.nn.gelu(x, approximate=True)

def _silu(x):
    return jax.nn.silu(x)

def _sigmoid(x):
    return jax.nn.sigmoid(x)

def _layernorm(x, axis=-1, eps=1e-05):
    m = jnp.mean(x, axis=axis, keepdims=True)
    v = jnp.var(x, axis=axis, keepdims=True)
    return (x - m) / jnp.sqrt(v + eps)

def _scatter_add(tgt, idx, src, axis=0):
    return tgt.at[idx].add(src)

def _segment_sum(src, seg, n):
    return jax.ops.segment_sum(src, seg, n)
kernel_name = 'mk_recurrent_d1_jaxref_r8_b737e2'

def setup_inputs(seed: int=0):
    np.random.seed(seed)
    _w = jnp.asarray

    def _L0_attn_setup():
        import jax, jax.numpy as jnp
        import numpy as np
        import math
        EMB = 256
        HEADS = 16
        HEAD_DIM = EMB // HEADS
        SCALE = math.sqrt(HEAD_DIM)

        def srms_norm(x, eps_min=1e-12):
            d = x.shape[-1]
            xf = x.astype(jnp.float32)
            norm = jnp.linalg.norm(xf * (1.0 / math.sqrt(d)), axis=-1, keepdims=True)
            norm = jnp.maximum(norm, eps_min)
            return (xf / norm).astype(x.dtype)
        key = jax.random.key(seed)
        ks = jax.random.split(key, 6)
        x = jax.random.normal(ks[0], (4, 512, EMB), dtype=jnp.float32)
        std = 1.0 / math.sqrt(EMB)
        Wq = jax.random.normal(ks[1], (EMB, EMB), dtype=jnp.float32) * std
        Wk = jax.random.normal(ks[2], (EMB, EMB), dtype=jnp.float32) * std
        Wv = jax.random.normal(ks[3], (EMB, EMB), dtype=jnp.float32) * std
        Wu = jax.random.normal(ks[4], (EMB, EMB), dtype=jnp.float32) * std
        Wo = jax.random.normal(ks[5], (EMB, EMB), dtype=jnp.float32) * std
        return {'x': x, 'Wq': Wq, 'Wk': Wk, 'Wv': Wv, 'Wu': Wu, 'Wo': Wo}
    _L0_attn_in = _L0_attn_setup()

    def _L0_ffn_setup():
        import jax, jax.numpy as jnp
        import numpy as np
        TOP_K = 4

        def _silu_and_mul(gu):
            g, u = jnp.split(gu, 2, axis=-1)
            return jax.nn.silu(g) * u
        key = jax.random.key(seed)
        ks = jax.random.split(key, 7)
        H, E, I, Is = (256, 16, 176, 704)
        s = 0.02
        return {'hidden_states': jax.random.normal(ks[0], (4, 128, H), dtype=jnp.float32), 'gate_w': jax.random.normal(ks[1], (E, H), dtype=jnp.float32) * s, 'sgate_w': jax.random.normal(ks[2], (1, H), dtype=jnp.float32) * s, 'w13': jax.random.normal(ks[3], (E, 2 * I, H), dtype=jnp.float32) * s, 'w2': jax.random.normal(ks[4], (E, H, I), dtype=jnp.float32) * s, 'shared_gate_up_w': jax.random.normal(ks[5], (2 * Is, H), dtype=jnp.float32) * s, 'shared_down_w': jax.random.normal(ks[6], (H, Is), dtype=jnp.float32) * s}
    _L0_ffn_in = _L0_ffn_setup()
    _d = {'L0_attn_x': _L0_attn_in['x'], 'L0_attn_Wq': _L0_attn_in['Wq'], 'L0_attn_Wk': _L0_attn_in['Wk'], 'L0_attn_Wv': _L0_attn_in['Wv'], 'L0_attn_Wu': _L0_attn_in['Wu'], 'L0_attn_Wo': _L0_attn_in['Wo'], 'L0_ffn_gate_w': _L0_ffn_in['gate_w'], 'L0_ffn_sgate_w': _L0_ffn_in['sgate_w'], 'L0_ffn_w13': _L0_ffn_in['w13'], 'L0_ffn_w2': _L0_ffn_in['w2'], 'L0_ffn_shared_gate_up_w': _L0_ffn_in['shared_gate_up_w'], 'L0_ffn_shared_down_w': _L0_ffn_in['shared_down_w']}
    _x0 = _d['L0_attn_x']
    _d['L0_attn_x'] = jax.random.normal(jax.random.fold_in(jax.random.key(seed), 1), (4, 1024, 256), dtype=_x0.dtype)
    del _x0
    return _d

def reference(L0_attn_x, L0_attn_Wq, L0_attn_Wk, L0_attn_Wv, L0_attn_Wu, L0_attn_Wo, L0_ffn_gate_w, L0_ffn_sgate_w, L0_ffn_w13, L0_ffn_w2, L0_ffn_shared_gate_up_w, L0_ffn_shared_down_w):

    def _L0_attn_ref(x, Wq, Wk, Wv, Wu, Wo):
        import jax, jax.numpy as jnp
        import numpy as np
        import math
        EMB = 256
        HEADS = 16
        HEAD_DIM = EMB // HEADS
        SCALE = math.sqrt(HEAD_DIM)

        def srms_norm(x, eps_min=1e-12):
            d = x.shape[-1]
            xf = x.astype(jnp.float32)
            norm = jnp.linalg.norm(xf * (1.0 / math.sqrt(d)), axis=-1, keepdims=True)
            norm = jnp.maximum(norm, eps_min)
            return (xf / norm).astype(x.dtype)
        B, L, D = x.shape
        H, dh = (HEADS, HEAD_DIM)
        q = (x @ Wq).reshape(B, L, H, dh).transpose(0, 2, 1, 3)
        k = (x @ Wk).reshape(B, L, H, dh).transpose(0, 2, 1, 3)
        v = (x @ Wv).reshape(B, L, H, dh).transpose(0, 2, 1, 3)
        u = (x @ Wu).reshape(B, L, H, dh).transpose(0, 2, 1, 3)
        q = jax.nn.relu(q) / SCALE
        k = jax.nn.relu(k) / SCALE
        u = jax.nn.silu(u)
        kv = jnp.einsum('bhlk,bhlv->bhkv', k, v)
        out = jnp.einsum('bhlk,bhkv->bhlv', q, kv)
        out = srms_norm(out) * u
        out = out.transpose(0, 2, 1, 3).reshape(B, L, D)
        return out @ Wo

    def _L0_ffn_ref(hidden_states, gate_w, sgate_w, w13, w2, shared_gate_up_w, shared_down_w):
        import jax, jax.numpy as jnp
        import numpy as np
        TOP_K = 4

        def _silu_and_mul(gu):
            g, u = jnp.split(gu, 2, axis=-1)
            return jax.nn.silu(g) * u
        B, S, H = hidden_states.shape
        x = hidden_states.reshape(-1, H)
        E = gate_w.shape[0]
        shared = _silu_and_mul(x @ shared_gate_up_w.T) @ shared_down_w.T
        shared = shared * jax.nn.sigmoid(x @ sgate_w.T)
        router_logits = x @ gate_w.T
        routing_weights = jax.nn.softmax(router_logits.astype(jnp.float32), axis=-1)
        topk_w, topk_ids = jax.lax.top_k(routing_weights, TOP_K)

        def body(acc, ew):
            w13_e, w2_e, e = ew
            coef = jnp.sum(jnp.where(topk_ids == e, topk_w, 0.0), axis=-1)
            h = _silu_and_mul(x @ w13_e.T)
            acc = acc + (h @ w2_e.T).astype(jnp.float32) * coef[:, None]
            return (acc, None)
        init = jnp.zeros((x.shape[0], H), dtype=jnp.float32)
        sparse_out, _ = jax.lax.scan(body, init, (w13, w2, jnp.arange(E)))
        out = shared + sparse_out.astype(x.dtype)
        return out.reshape(B, S, H)
    x = L0_attn_x
    xn = _layernorm(x, axis=-1)
    s = _L0_attn_ref(xn, L0_attn_Wq, L0_attn_Wk, L0_attn_Wv, L0_attn_Wu, L0_attn_Wo)
    g = _silu(_L0_ffn_ref(xn, L0_ffn_gate_w, L0_ffn_sgate_w, L0_ffn_w13, L0_ffn_w2, L0_ffn_shared_gate_up_w, L0_ffn_shared_down_w))
    x = x + s * g
    return x

_drawn_inputs = setup_inputs


def setup_inputs(seed=0):
    import zlib

    import numpy as np

    out = dict(_drawn_inputs(seed))
    spreads = {}
    factors = {'L0_attn_Wq': 8.0,
     'L0_attn_Wk': 8.0,
     'L0_attn_Wv': 8.0,
     'L0_attn_Wu': 8.0,
     'L0_attn_Wo': 8.0,
     'L0_ffn_gate_w': 8.0,
     'L0_ffn_sgate_w': 8.0,
     'L0_ffn_w13': 8.0,
     'L0_ffn_w2': 8.0,
     'L0_ffn_shared_gate_up_w': 8.0,
     'L0_ffn_shared_down_w': 8.0}
    for name, (base, spread) in spreads.items():
        noise = np.random.default_rng([zlib.crc32(name.encode()), seed]).standard_normal(out[name].shape)
        drawn = base * np.exp(spread * noise) if base else spread * noise
        out[name] = jnp.asarray(drawn.astype(out[name].dtype))
    for name, factor in factors.items():
        out[name] = (out[name] * factor).astype(out[name].dtype)
    return out
```

```python
from contextlib import ExitStack

import concourse.bass as bass
from concourse import mybir

ALU = mybir.AluOpType
ACT = mybir.ActivationFunctionType
AX = mybir.AxisListType
F32 = mybir.dt.float32
R32 = mybir.dt.float32r
I32 = mybir.dt.int32

P = 128
H = 256
KC = H // P
T = 256
S = T // P
HEAD = 16
E = 16
I = 176
SHARED = 4
NE = E + SHARED
IR = I - P
EPS = 1e-5
NONE = -3.0e38
MAGIC = float(0x5F3759DF)

CK, CV, CU, CG, CQ = 0, 256, 512, 768, 786
NG = CQ - CG
NPROJ = CQ + 256
NUP = 3 * P
CD = KC * NUP
NW = CD + 2 * H


def build(nc, x, wproj, wo, wffn, consts, out):
    NT = out.shape[0] // P
    NU = NT // S
    NB = 4
    UB = NU // NB
    TB = UB * S

    with ExitStack() as top:
        def psum(name, ctx):
            return ctx.enter_context(nc.psum_tensor(name, [P, 512], F32))

        def sem(name, ctx):
            return ctx.enter_context(nc.semaphore(name))

        def sb(name, shape, dt, ctx):
            return ctx.enter_context(nc.sbuf_tensor(name, shape, dt))

        xT_hi = sb("xT_hi", [P, KC, NU * T], R32, top)
        xT_lo = sb("xT_lo", [P, KC, NU * T], R32, top)
        s_sb = sb("s_sb", [P, NT, H], F32, top)
        coef = sb("coef", [P, NT, NE], F32, top)

        x_v = x.rearrange("(n s p) h -> n p s h", s=S, p=P)
        out_v = out.rearrange("(n s p) h -> n p s h", s=S, p=P)

        attention(nc, top, sb, psum, sem, x_v, wproj, wo, consts, xT_hi, xT_lo, s_sb, coef, NT, NB, UB, TB)
        with ExitStack() as mid:
            acc = sb("acc", [P, NT, H], F32, mid)
            experts(nc, sb, psum, sem, wffn, xT_hi, xT_lo, coef, acc, NU)
            finish(nc, sb, sem, x_v, s_sb, acc, out_v, NU)


def rsqrt_steps(nc, link, v, vh, i32, y, t):
    link(nc.vector.tensor_scalar(i32, v.bitcast(I32), 1, None, ALU.logical_shift_right))
    nc.vector.tensor_scalar(vh, v, -0.5, None, ALU.mult)
    link(nc.vector.tensor_scalar(y.bitcast(I32), i32, -1.0, MAGIC, ALU.mult, ALU.add))
    for _ in range(4):
        link(nc.vector.tensor_tensor(t, vh, y, ALU.mult))
        link(nc.vector.tensor_tensor(t, t, y, ALU.mult))
        link(nc.vector.scalar_tensor_tensor(out=y, in0=t, scalar=1.5, in1=y, op0=ALU.add, op1=ALU.mult))


RSQRT_LINKS = 14


def attention(nc, top, sb, psum, sem, x_v, wproj, wo, consts, xT_hi, xT_lo, s_sb, coef, NT, NB, UB, TB):
    with ExitStack() as ctx:
        ident = sb("ident", [P, P], F32, ctx)
        mask = sb("mask", [P, P], F32, ctx)
        wp_raw = sb("wp_raw", [P, KC * NPROJ], F32, ctx)
        wp_hi = sb("wp_hi", [P, KC, NPROJ], R32, ctx)
        wp_lo = sb("wp_lo", [P, KC, NPROJ], R32, ctx)
        wo_raw = sb("wo_raw", [P, KC * H], F32, ctx)
        wo_hi = sb("wo_hi", [P, KC, H], R32, ctx)
        wo_lo = sb("wo_lo", [P, KC, H], R32, ctx)
        xin = sb("xin", [P, 2, S, H], F32, ctx)
        xn = sb("xn", [P, 2, S, H], F32, ctx)
        xs_hi = sb("xs_hi", [P, 2, KC, T], R32, ctx)
        xs_lo = sb("xs_lo", [P, 2, KC, T], R32, ctx)
        stats = sb("stats", [P, S, 6], F32, ctx)
        mv = sb("mv", [P, S, 2], F32, ctx)
        var = sb("var", [P, S], F32, ctx)
        varh = sb("varh", [P, S], F32, ctx)
        vari = sb("vari", [P, S], I32, ctx)
        rstd = sb("rstd", [P, S], F32, ctx)
        vart = sb("vart", [P, S], F32, ctx)
        k_hi = sb("k_hi", [P, S, H], R32, ctx)
        k_lo = sb("k_lo", [P, S, H], R32, ctx)
        v_hi = sb("v_hi", [P, S, H], R32, ctx)
        v_lo = sb("v_lo", [P, S, H], R32, ctx)
        q_hi = sb("q_hi", [P, KC, UB * T], R32, ctx)
        q_lo = sb("q_lo", [P, KC, UB * T], R32, ctx)
        kvm = sb("kvm", [P, KC, P], F32, ctx)
        kv_hi = sb("kv_hi", [P, KC, P], R32, ctx)
        kv_lo = sb("kv_lo", [P, KC, P], R32, ctx)
        u_sb = sb("u_sb", [P, TB, H], F32, ctx)
        sq = sb("sq", [P, 2, H], F32, ctx)
        ms = sb("ms", [P, TB * HEAD], F32, ctx)
        msh = sb("msh", [P, TB * HEAD], F32, ctx)
        msi = sb("msi", [P, TB * HEAD], I32, ctx)
        mst = sb("mst", [P, TB * HEAD], F32, ctx)
        rn = sb("rn", [P, TB * HEAD], F32, ctx)
        at = sb("at", [P, 2, H], F32, ctx)
        aT_hi = sb("aT_hi", [P, 2, KC, P], R32, ctx)
        aT_lo = sb("aT_lo", [P, 2, KC, P], R32, ctx)
        lg = sb("lg", [P, TB, 25], F32, ctx)
        top8 = sb("top8", [P, TB, 8], F32, ctx)
        rp = sb("rp", [P, TB, 24], F32, ctx)
        lga = sb("lga", [P, NT, 17], F32, ctx)
        rpa = sb("rpa", [P, NT, E], F32, ctx)
        lmax = sb("lmax", [P, NT], F32, ctx)
        ex = sb("ex", [P, NT, E], F32, ctx)
        den = sb("den", [P, NT], F32, ctx)
        gt = sb("gt", [P, NT], F32, ctx)

        psX = psum("psX", ctx)
        psKV = [psum(f"psKV{i}", ctx) for i in range(2)]
        psUG = [psum(f"psUG{i}", ctx) for i in range(2)]
        psQ = psum("psQ", ctx)
        psA = [psum(f"psA{i}", ctx) for i in range(2)]
        psT = [psX, psQ]

        s_w = sem("a_w", ctx)
        w_hi_done = sem("a_w_hi", ctx)
        w_done = sem("a_w_done", ctx)
        x_in = [sem(f"a_x_in{i}", ctx) for i in range(2)]
        x_copied = [sem(f"a_x_copied{i}", ctx) for i in range(2)]
        xn_ready = sem("a_xn_ready", ctx)
        xT_ps = sem("a_xT_ps", ctx)
        xh_ready = sem("a_xh_ready", ctx)
        xs_ready = sem("a_xs_ready", ctx)
        kv_ps = sem("a_kv_ps", ctx)
        kvh_ready = sem("a_kvh_ready", ctx)
        kvl_ready = sem("a_kvl_ready", ctx)
        ug_ps = sem("a_ug_ps", ctx)
        u_ready = sem("a_u_ready", ctx)
        q_ps = sem("a_q_ps", ctx)
        qh_ready = sem("a_qh_ready", ctx)
        unit_out = sem("a_unit_out", ctx)
        kva_ps = sem("a_kva_ps", ctx)
        kvb_ready = sem("a_kvb_ready", ctx)
        o_ps = sem("a_o_ps", ctx)
        sq_ready = sem("a_sq_ready", ctx)
        p_done = sem("a_p_done", ctx)
        at_ready = sem("a_at_ready", ctx)
        aT_ps = sem("a_aT_ps", ctx)
        ah_ready = sem("a_ah_ready", ctx)
        as_ready = sem("a_as_ready", ctx)
        s_ps = sem("a_s_ps", ctx)
        s_done = sem("a_s_done", ctx)
        d_ready = sem("a_d_ready", ctx)
        ex_ready = sem("a_ex_ready", ctx)
        dve_own = sem("a_dve_own", ctx)
        dve_passed = sem("a_dve_passed", ctx)

        def f32(ap):
            return ap.bitcast(F32)

        with nc.Block() as block:

            @block.sync
            def _(sp):
                for p in range(2):
                    sp.sem_inc(x_copied[p], 16)
                sp.dma_start(ident[:, :], consts[:, 0:P]).then_inc(s_w, 16)
                sp.dma_start(xin[:, 0], x_v[0]).then_inc(x_in[0], 16)
                sp.dma_start(wp_raw[:, :], wproj).then_inc(s_w, 16)
                sp.dma_start(xin[:, 1], x_v[1]).then_inc(x_in[1], 16)
                sp.dma_start(mask[:, :], consts[:, P:2 * P]).then_inc(s_w, 16)
                sp.dma_start(wo_raw[:, :], wo).then_inc(s_w, 16)
                with sp.Fori(0, NB) as b:
                    for u in range(UB):
                        n, p = b * UB + u, u % 2
                        sp.wait_ge(xs_ready, n + 1)
                        sp.dma_start(f32(xT_hi[:, :, bass.ds(n * T, T)]), f32(xs_hi[:, p])).then_inc(x_copied[p], 16)
                        sp.dma_start(f32(xT_lo[:, :, bass.ds(n * T, T)]), f32(xs_lo[:, p])).then_inc(x_copied[p], 16)
                        sp.wait_ge(xn_ready, n + 1)
                        sp.dma_start(xin[:, p], x_v[bass.ds(n + 2, 1)].rearrange("o p s h -> p (o s) h")).then_inc(x_in[p], 16)
                for p in range(2):
                    sp.wait_ge(x_copied[p], 32 * (NB * UB // 2) + 16)
                    sp.wait_ge(x_in[p], 16 * (NB * UB // 2 + 1))

            @block.scalar
            def _(act):
                nc.scalar.sem_inc(s_done, 1)
                act.wait_ge(s_w, 64)
                nc.scalar.copy(wp_hi[:, :, :].rearrange("p k n -> p (k n)"), wp_raw[:, :])
                nc.scalar.copy(wo_hi[:, :, :].rearrange("p k n -> p (k n)"), wo_raw[:, :]).then_inc(w_hi_done, 1)
                act.wait_ge(xT_ps, 1)
                nc.scalar.copy(xs_hi[:, 0].rearrange("p k t -> p (k t)"), psX[:, :]).then_inc(xh_ready, 1)
                with act.Fori(0, NB) as b:
                    for u in range(UB):
                        n, p = b * UB + u, u % 2
                        for s in range(S):
                            act.wait_ge(kv_ps, n * S + s + 1)
                            nc.scalar.activation(k_hi[:, s], psKV[s][:, 0:H], ACT.Relu)
                            nc.scalar.copy(v_hi[:, s], psKV[s][:, H:2 * H]).then_inc(kvh_ready, 1)
                        act.wait_ge(xT_ps, n + 2)
                        act.wait_ge(x_copied[1 - p], b * (32 * UB // 2) + 32 * ((u + 1) // 2) + 16)
                        nc.scalar.copy(xs_hi[:, 1 - p].rearrange("p k t -> p (k t)"), psX[:, :]).then_inc(xh_ready, 1)
                        for s in range(S):
                            act.wait_ge(ug_ps, n * S + s + 1)
                            nc.scalar.activation(u_sb[:, u * S + s, :], psUG[s][:, 0:H], ACT.Silu).then_inc(u_ready, 1)
                        act.wait_ge(q_ps, n + 1)
                        nc.scalar.activation(q_hi[:, :, u * T:(u + 1) * T],
                                             psQ[:, :].rearrange("p (k t) -> p k t", k=KC), ACT.Relu).then_inc(qh_ready, 1)
                    for t in range(TB):
                        act.wait_ge(o_ps, b * TB + t + 1)
                        nc.scalar.activation(sq[:, t % 2], psKV[t % 2][:, 0:H], ACT.Square).then_inc(sq_ready, 1)

                    def head_out(t):
                        act.wait_ge(s_ps, b * TB + t + 1)
                        nc.scalar.copy(s_sb[:, bass.ds(b * TB + t, 1), :].rearrange("p o h -> p (o h)"),
                                       psUG[t % 2][:, 0:H]).then_inc(s_done, 1)

                    for t in range(TB):
                        act.wait_ge(aT_ps, b * TB + t + 1)
                        nc.scalar.copy(aT_hi[:, t % 2].rearrange("p k t -> p (k t)"), psT[t % 2][:, 0:H]).then_inc(ah_ready, 1)
                        if t:
                            head_out(t - 1)
                    head_out(TB - 1)
                act.wait_ge(d_ready, 1)
                nc.scalar.activation(ex[:, :, :], ex[:, :, :], ACT.Exp)
                nc.scalar.activation(gt[:, :], lga[:, :, 0], ACT.Tanh, scale=0.5).then_inc(ex_ready, 1)

            @block.vector
            def _(dve):
                count = [0, 0]

                def link(ins):
                    ins.then_inc(dve_own, 1)
                    count[1] += 1
                    dve.wait_ge(dve_own, count[0] + count[1])

                def normalise(m_in, p):
                    dve.wait_ge(x_in[p], m_in)
                    for s in range(S):
                        last = nc.vector.bn_stats(stats[:, s, :], xin[:, p, s, :])
                    link(last)
                    dve.sem_inc(dve_passed, 1)
                    for s in range(S):
                        last = nc.vector.bn_aggr(mv[:, s, :], stats[:, s, :])
                    link(last)
                    link(nc.vector.tensor_scalar(var[:, :], mv[:, :, 1], EPS, None, ALU.add))
                    rsqrt_steps(nc, link, var[:, :], varh[:, :], vari[:, :], rstd[:, :], vart[:, :])
                    for s in range(S):
                        last = nc.vector.tensor_scalar(xn[:, p, s, :], xin[:, p, s, :], mv[:, s, 0:1],
                                                       rstd[:, s:s + 1], ALU.subtract, ALU.mult)
                    last.then_inc(xn_ready, 1)

                def split_x(p):
                    nc.vector.tensor_tensor(xs_lo[:, p].rearrange("p k t -> p (k t)"), psX[:, :],
                                            f32(xs_hi[:, p].rearrange("p k t -> p (k t)")), ALU.subtract).then_inc(xs_ready, 1)

                nc.vector.sem_inc(unit_out, 1)
                nc.vector.memset(lg[:, :, :], NONE)
                normalise(16, 0)
                dve.wait_ge(w_hi_done, 1)
                nc.vector.tensor_tensor(wp_lo[:, :, :].rearrange("p k n -> p (k n)"), wp_raw[:, :],
                                        f32(wp_hi[:, :, :].rearrange("p k n -> p (k n)")), ALU.subtract)
                nc.vector.tensor_tensor(wo_lo[:, :, :].rearrange("p k n -> p (k n)"), wo_raw[:, :],
                                        f32(wo_hi[:, :, :].rearrange("p k n -> p (k n)")), ALU.subtract).then_inc(w_done, 1)
                dve.wait_ge(xh_ready, 1)
                split_x(0)
                normalise(16, 1)
                LINKS0 = count[1]
                links_per_seq = UB * (3 + RSQRT_LINKS) + 2 + (1 + RSQRT_LINKS) + 1 + 3
                with dve.Fori(0, NB) as b:
                    count[0], count[1] = LINKS0 + b * links_per_seq, 0
                    for u in range(UB):
                        n, p = b * UB + u, u % 2
                        for s in range(S):
                            dve.wait_ge(kvh_ready, n * S + s + 1)
                            nc.vector.scalar_tensor_tensor(out=k_lo[:, s], in0=psKV[s][:, 0:H], scalar=0.0,
                                                           in1=f32(k_hi[:, s]), op0=ALU.max, op1=ALU.subtract)
                            nc.vector.tensor_tensor(v_lo[:, s], psKV[s][:, H:2 * H], f32(v_hi[:, s]),
                                                    ALU.subtract).then_inc(kvl_ready, 1)
                        dve.wait_ge(xh_ready, n + 2)
                        split_x(1 - p)
                        for s in range(S):
                            dve.wait_ge(u_ready, n * S + s + 1)
                            nc.vector.tensor_copy(lg[:, u * S + s, 0:17], psUG[s][:, H:H + 17])
                        dve.wait_ge(qh_ready, n + 1)
                        nc.vector.scalar_tensor_tensor(out=q_lo[:, :, u * T:(u + 1) * T],
                                                       in0=psQ[:, :].rearrange("p (k t) -> p k t", k=KC), scalar=0.0,
                                                       in1=f32(q_hi[:, :, u * T:(u + 1) * T]),
                                                       op0=ALU.max, op1=ALU.subtract).then_inc(unit_out, 1)
                        normalise(b * (16 * UB // 2) + 16 * (u // 2 + 2), p)
                    dve.wait_ge(kva_ps, b + 1)
                    for c in range(KC):
                        last = nc.vector.tensor_tensor(kvm[:, c], psA[c][:, 0:P], mask[:, :], ALU.mult)
                    link(last)
                    link(nc.vector.tensor_copy(kv_hi[:, :, :], kvm[:, :, :]))
                    nc.vector.tensor_tensor(kv_lo[:, :, :], kvm[:, :, :], f32(kv_hi[:, :, :]), ALU.subtract).then_inc(kvb_ready, 1)
                    for t in range(TB):
                        dve.wait_ge(sq_ready, b * TB + t + 1)
                        last = nc.vector.tensor_reduce(ms[:, t * HEAD:(t + 1) * HEAD],
                                                       sq[:, t % 2].rearrange("p (h d) -> p h d", d=HEAD), AX.X, ALU.add)
                        nc.vector.tensor_tensor(u_sb[:, t, :], psKV[t % 2][:, 0:H], u_sb[:, t, :], ALU.mult).then_inc(p_done, 1)
                        if t == TB - 1:
                            dve.wait_ge(p_done, b * TB + TB)
                    link(nc.vector.tensor_scalar(ms[:, :], ms[:, :], 1.0 / HEAD, 1e-24, ALU.mult, ALU.max))
                    rsqrt_steps(nc, link, ms[:, :], msh[:, :], msi[:, :], rn[:, :], mst[:, :])

                    def split_a(t):
                        dve.wait_ge(ah_ready, b * TB + t + 1)
                        nc.vector.tensor_tensor(aT_lo[:, t % 2].rearrange("p k t -> p (k t)"), psT[t % 2][:, 0:H],
                                                f32(aT_hi[:, t % 2].rearrange("p k t -> p (k t)")),
                                                ALU.subtract).then_inc(as_ready, 1)

                    for t in range(TB):
                        if t >= 2:
                            dve.wait_ge(aT_ps, b * TB + t - 1)
                        nc.vector.tensor_tensor(
                            at[:, t % 2].rearrange("p (h d) -> p h d", d=HEAD),
                            u_sb[:, t, :].rearrange("p (h d) -> p h d", d=HEAD),
                            rn[:, t * HEAD:(t + 1) * HEAD].unsqueeze(2).broadcast_to([P, HEAD, HEAD]),
                            ALU.mult).then_inc(at_ready, 1)
                        if t:
                            split_a(t - 1)
                    split_a(TB - 1)
                    for t in range(TB):
                        last = nc.vector.max(top8[:, t, :], lg[:, t, 1:17])
                    link(last)
                    link(nc.vector.memset(top8[:, :, 4:8], NONE))
                    dve.sem_inc(dve_passed, 1)
                    for t in range(TB):
                        last = nc.vector.match_replace(rp[:, t, :], top8[:, t, :], lg[:, t, 1:25], NONE)
                    link(last)
                    nc.vector.tensor_copy(lga[:, bass.ds(b * TB, TB), :], lg[:, :, 0:17])
                    link(nc.vector.tensor_copy(rpa[:, bass.ds(b * TB, TB), :], rp[:, :, 0:E]))
                    assert count[1] == links_per_seq, count[1]
                count[0], count[1] = LINKS0 + NB * links_per_seq, 0
                lgr = lga[:, :, 1:17]
                link(nc.vector.tensor_reduce(lmax[:, :], lgr, AX.X, ALU.max))
                nc.vector.tensor_tensor(ex[:, :, :], lgr, lmax[:, :].unsqueeze(2).broadcast_to([P, NT, E]),
                                        ALU.subtract).then_inc(d_ready, 1)
                nc.vector.tensor_tensor(rpa[:, :, :], rpa[:, :, :], lgr, ALU.not_equal)
                dve.wait_ge(ex_ready, 1)
                link(nc.vector.tensor_reduce(den[:, :], ex[:, :, :], AX.X, ALU.add))
                link(nc.vector.reciprocal(den[:, :], den[:, :]))
                link(nc.vector.tensor_tensor(ex[:, :, :], ex[:, :, :], rpa[:, :, :], ALU.mult))
                nc.vector.tensor_tensor(coef[:, :, 0:E], ex[:, :, :], den[:, :].unsqueeze(2).broadcast_to([P, NT, E]), ALU.mult)
                for j in range(SHARED):
                    nc.vector.tensor_scalar(coef[:, :, E + j], gt[:, :], 0.5, 0.5, ALU.mult, ALU.add)

            @block.tensor
            def _(pe):
                def transpose_x(p):
                    for k in range(KC):
                        for s in range(S):
                            last = nc.tensor.transpose(psX[:, k * T + s * P:k * T + (s + 1) * P],
                                                       xn[:, p, s, k * P:(k + 1) * P], ident[:, :])
                    last.then_inc(xT_ps, 1)

                def products(out, lhs, rhs):
                    i = 0
                    for k in range(len(lhs)):
                        (ah, al), (bh, bl) = lhs[k], rhs[k]
                        for a, c in ((ah, bh), (ah, bl), (al, bh)):
                            last = nc.tensor.matmul(out, a, c, start=i == 0, stop=i == 3 * len(lhs) - 1)
                            i += 1
                    return last

                def wcols(k, a, n):
                    return wp_hi[:, k, a:a + n], wp_lo[:, k, a:a + n]

                pe.wait_ge(s_w, 64)
                pe.wait_ge(xn_ready, 1)
                transpose_x(0)
                pe.wait_ge(w_done, 1)
                with pe.Fori(0, NB) as b:
                    for u in range(UB):
                        n, p = b * UB + u, u % 2

                        def xcols(k, a, n):
                            return xs_hi[:, p, k, a:a + n], xs_lo[:, p, k, a:a + n]

                        pe.wait_ge(xs_ready, n + 1)
                        for s in range(S):
                            products(psKV[s][:, :], [xcols(k, s * P, P) for k in range(KC)],
                                     [wcols(k, CK, 2 * H) for k in range(KC)]).then_inc(kv_ps, 1)
                        pe.wait_ge(xn_ready, n + 2)
                        transpose_x(1 - p)
                        pe.wait_ge(unit_out, n + 1)
                        if u == 0:
                            pe.wait_ge(s_done, b * TB + 1)
                        for s in range(S):
                            for k in range(KC):
                                (xh, xl), (wh, wl) = xcols(k, s * P, P), wcols(k, CU, H + NG)
                                nc.tensor.matmul(psUG[s][:, 0:H + NG], xh, wh, start=k == 0, stop=False)
                                nc.tensor.matmul(psUG[s][:, 0:H + NG], xh, wl, start=False, stop=False)
                                nc.tensor.matmul(psUG[s][:, H:H + NG], xl, wl[:, H:H + NG], start=False, stop=False,
                                                 skip_group_check=True)
                                last = nc.tensor.matmul(psUG[s][:, 0:H + NG], xl, wh, start=False, stop=k == KC - 1)
                            last.then_inc(ug_ps, 1)
                        for c in range(KC):
                            last = products(psQ[:, c * T:(c + 1) * T], [wcols(k, CQ + c * P, P) for k in range(KC)],
                                            [xcols(k, 0, T) for k in range(KC)])
                        last.then_inc(q_ps, 1)
                        pe.wait_ge(kvl_ready, n * S + S)
                        for s in range(S):
                            for c in range(KC):
                                kk = slice(c * P, (c + 1) * P)
                                for i, (a, v) in enumerate(((k_hi, v_hi), (k_hi, v_lo), (k_lo, v_hi))):
                                    last = nc.tensor.matmul(psA[c][:, 0:P], a[:, s, kk], v[:, s, kk],
                                                            start=u == 0 and s == 0 and i == 0,
                                                            stop=u == UB - 1 and s == S - 1 and i == 2)
                    last.then_inc(kva_ps, 1)
                    pe.wait_ge(kvb_ready, b + 1)
                    for t in range(TB):
                        if t >= 2:
                            pe.wait_ge(p_done, b * TB + t - 1)
                        for c in range(KC):
                            last = products(psKV[t % 2][:, c * P:(c + 1) * P],
                                            [(q_hi[:, c, t * P:(t + 1) * P], q_lo[:, c, t * P:(t + 1) * P])],
                                            [(kv_hi[:, c], kv_lo[:, c])])
                        last.then_inc(o_ps, 1)

                    def head_out(t):
                        pe.wait_ge(as_ready, b * TB + t + 1)
                        if t >= 2:
                            pe.wait_ge(s_done, b * TB + t)
                        products(psUG[t % 2][:, 0:H], [(aT_hi[:, t % 2, k], aT_lo[:, t % 2, k]) for k in range(KC)],
                                 [(wo_hi[:, k], wo_lo[:, k]) for k in range(KC)]).then_inc(s_ps, 1)

                    for t in range(TB):
                        pe.wait_ge(at_ready, b * TB + t + 1)
                        for k in range(KC):
                            last = nc.tensor.transpose(psT[t % 2][:, k * P:(k + 1) * P], at[:, t % 2, k * P:(k + 1) * P],
                                                       ident[:, :])
                        last.then_inc(aT_ps, 1)
                        if t:
                            head_out(t - 1)
                    head_out(TB - 1)


def experts(nc, sb, psum, sem, wffn, xT_hi, xT_lo, coef, acc, NU):
    with ExitStack() as ctx:
        w_raw = sb("w_raw", [P, 2, NW], F32, ctx)
        w_hi = sb("w_hi", [P, 2, NW], R32, ctx)
        w_lo = sb("w_lo", [P, 2, NW], R32, ctx)
        sg0 = sb("sg0", [P, T], F32, ctx)
        sgm = sb("sgm", [P, T], F32, ctx)
        h0 = sb("h0", [P, T], F32, ctx)
        hm = sb("hm", [P, T], F32, ctx)
        h0_hi = sb("h0_hi", [P, T], R32, ctx)
        h0_lo = sb("h0_lo", [P, T], R32, ctx)
        hm_s = sb("hm_s", [P, T], R32, ctx)

        psG = psum("psG", ctx)
        psM = psum("psM", ctx)
        psU = psum("psU", ctx)
        psD = psum("psD", ctx)

        w_in = [sem(f"e_w_in{i}", ctx) for i in range(2)]
        zeroed = sem("e_zeroed", ctx)
        pool_passed = sem("e_pool_passed", ctx)
        wh_done = sem("e_wh_done", ctx)
        w_ready = sem("e_w_ready", ctx)
        up_ps = sem("e_up_ps", ctx)
        sg_ready = sem("e_sg_ready", ctx)
        h_done = sem("e_h_done", ctx)
        hh_ready = sem("e_hh_ready", ctx)
        hl_ready = sem("e_hl_ready", ctx)
        d_ps = sem("e_d_ps", ctx)
        acc_done = sem("e_acc_done", ctx)
        HALF = P // 2

        def f32(ap):
            return ap.bitcast(F32)

        with nc.Block() as block:

            @block.sync
            def _(sp):
                for p in range(2):
                    sp.dma_start(w_raw[:, p], wffn[p]).then_inc(w_in[p], 16)
                with sp.Fori(0, NE // 2 - 1) as e2:
                    for p in range(2):
                        e = e2 * 2 + p
                        sp.wait_ge(w_ready, e + 1)
                        sp.dma_start(w_raw[:, p], wffn[bass.ds(e + 2, 1)].rearrange("o p n -> p (o n)")).then_inc(w_in[p], 16)

            @block.gpsimd
            def _(pool):
                for p in range(2):
                    last = nc.gpsimd.memset(f32(w_lo[HALF:P, p, CD + H:NW]), 0.0)
                last.then_inc(zeroed, 1)
                pool.wait_ge(zeroed, 1)

                with pool.Fori(0, NE // 2) as e2:
                    for p in range(2):
                        e = e2 * 2 + p
                        pool.wait_ge(w_in[p], e2 * 16 + 16)
                        pool.wait_ge(d_ps, e * NU + 1)
                        pool.sem_inc(pool_passed, 1)
                        nc.gpsimd.tensor_copy(w_hi[:, p], w_raw[:, p]).then_inc(wh_done, 1)
                        pool.wait_ge(wh_done, e + 1)
                        nc.gpsimd.tensor_tensor(w_lo[:, p, 0:CD + H], w_raw[:, p, 0:CD + H], f32(w_hi[:, p, 0:CD + H]), ALU.subtract)
                        nc.gpsimd.tensor_tensor(w_lo[0:HALF, p, CD + H:NW], w_raw[0:HALF, p, CD + H:NW],
                                                f32(w_hi[0:HALF, p, CD + H:NW]), ALU.subtract).then_inc(w_ready, 1)

            @block.scalar
            def _(act):
                with act.Fori(0, NE) as e:
                    with act.Fori(0, NU) as t:
                        g = e * NU + t
                        act.wait_ge(up_ps, g * 3 + 1)
                        nc.scalar.activation(sg0[:, :], psG[:, 0:T], ACT.Silu).then_inc(sg_ready, 1)
                        act.wait_ge(up_ps, g * 3 + 2)
                        nc.scalar.activation(sgm[0:HALF, :], psM[0:HALF, 0:T], ACT.Silu).then_inc(sg_ready, 1)
                        act.wait_ge(h_done, g + 2)
                        act.wait_ge(d_ps, g + NU + 1)
                        nc.scalar.copy(h0_hi[:, :], h0[:, :])
                        nc.scalar.copy(hm_s[0:HALF, :], hm[0:HALF, :]).then_inc(hh_ready, 1)

            @block.vector
            def _(dve):
                nc.vector.memset(acc[:, :, :], 0.0).then_inc(acc_done, 1)
                dve.wait_ge(acc_done, 1)
                nc.vector.sem_inc(h_done, 1)
                nc.vector.sem_inc(hl_ready, 1)

                def hidden(g):
                    dve.wait_ge(up_ps, g * 3 + 3)
                    dve.wait_ge(sg_ready, g * 2 + 2)
                    dve.wait_ge(hl_ready, g + 1)
                    nc.vector.tensor_tensor(h0[:, :], psU[:, 0:T], sg0[:, :], ALU.mult)
                    nc.vector.tensor_tensor(hm[0:HALF, :], psM[HALF:P, 0:T], sgm[0:HALF, :], ALU.mult).then_inc(h_done, 1)
                    dve.wait_ge(hh_ready, g + 1)
                    nc.vector.tensor_tensor(h0_lo[:, :], h0[:, :], f32(h0_hi[:, :]), ALU.subtract)
                    nc.vector.tensor_tensor(hm_s[HALF:P, :], hm[0:HALF, :], f32(hm_s[0:HALF, :]), ALU.subtract).then_inc(hl_ready, 1)

                def accumulate(e, t):
                    dve.wait_ge(d_ps, e * NU + t + 2 + NU)
                    for s in range(S):
                        a = acc[:, bass.ds(t * S + s, 1), :].rearrange("p o h -> p (o h)")
                        last = nc.vector.scalar_tensor_tensor(
                            out=a, in0=psD[:, s * H:(s + 1) * H],
                            scalar=coef[:, bass.ds(t * S + s, 1), bass.ds(e, 1)].rearrange("p o c -> p (o c)"),
                            in1=a, op0=ALU.mult, op1=ALU.add)
                    last.then_inc(acc_done, 1)

                with dve.Fori(0, NE) as e:
                    hidden(e * NU)
                    with dve.Fori(1, NU) as t:
                        hidden(e * NU + t)
                        accumulate(e, t - 1)
                    accumulate(e, NU - 1)

            @block.tensor
            def _(pe):
                pe.sem_inc(d_ps, NU + 1)
                with pe.Fori(0, NE // 2) as e2:
                    for p in range(2):
                        e = e2 * 2 + p

                        def up(t):
                            g = e * NU + t
                            pe.wait_ge(h_done, g + 1)
                            for c, bank in enumerate((psG, psM, psU)):
                                i = 0
                                for k in range(KC):
                                    a = k * NUP + c * P
                                    xc = (slice(None), k, bass.ds(t * T, T))
                                    for w, xx in ((w_hi, xT_hi), (w_hi, xT_lo), (w_lo, xT_hi)):
                                        last = nc.tensor.matmul(bank[:, 0:T], w[:, p, a:a + P], xx[xc], start=i == 0, stop=i == 5)
                                        i += 1
                                last.then_inc(up_ps, 1)

                        def down(t):
                            g = e * NU + t
                            pe.wait_ge(hl_ready, g + 2)
                            pe.wait_ge(acc_done, g + 1)
                            d0, d1 = slice(CD, CD + H), slice(CD + H, NW)
                            for s in range(S):
                                ss = slice(s * P, (s + 1) * P)
                                ops = ((h0_hi, w_hi, d0), (h0_hi, w_lo, d0), (h0_lo, w_hi, d0),
                                       (hm_s, w_hi, d1), (hm_s, w_lo, d1))
                                for i, (hh, w, d) in enumerate(ops):
                                    last = nc.tensor.matmul(psD[:, s * H:(s + 1) * H], hh[:, ss], w[:, p, d],
                                                            start=i == 0, stop=i == len(ops) - 1)
                            last.then_inc(d_ps, 1)

                        pe.wait_ge(w_ready, e + 1)
                        up(0)
                        with pe.Fori(1, NU) as t:
                            up(t)
                            down(t - 1)
                        down(NU - 1)


def finish(nc, sb, sem, x_v, s_sb, acc, out_v, NU):
    with ExitStack() as ctx:
        xf = sb("xf", [P, 2, S, H], F32, ctx)
        fg = sb("fg", [P, 2, S, H], F32, ctx)
        y = sb("y", [P, 2, S, H], F32, ctx)
        x_in = [sem(f"f_x_in{i}", ctx) for i in range(2)]
        y_out = [sem(f"f_y_out{i}", ctx) for i in range(2)]
        fg_ready = sem("f_fg_ready", ctx)
        prod = sem("f_prod", ctx)
        y_ready = sem("f_y_ready", ctx)
        with nc.Block() as block:

            @block.sync
            def _(sp):
                for p in range(2):
                    sp.sem_inc(y_out[p], 16)
                    sp.dma_start(xf[:, p], x_v[p]).then_inc(x_in[p], 16)
                with sp.Fori(0, NU // 2) as n2:
                    for p in range(2):
                        n = n2 * 2 + p
                        sp.wait_ge(y_ready, n + 3)
                        sp.dma_start(out_v[bass.ds(n, 1)].rearrange("o p s h -> p (o s) h"), y[:, p]).then_inc(y_out[p], 16)
                        sp.dma_start(xf[:, p], x_v[bass.ds(n + 2, 1)].rearrange("o p s h -> p (o s) h")).then_inc(x_in[p], 16)
                for p in range(2):
                    sp.wait_ge(y_out[p], 16 * (NU // 2) + 16)
                    sp.wait_ge(x_in[p], 16 * (NU // 2 + 1))

            @block.scalar
            def _(act):
                with act.Fori(0, NU // 2) as n2:
                    for p in range(2):
                        n = n2 * 2 + p
                        act.wait_ge(y_ready, n + 1)
                        nc.scalar.activation(fg[:, p], acc[:, bass.ds(n * S, S), :], ACT.Silu).then_inc(fg_ready, 1)

            @block.vector
            def _(dve):
                nc.vector.sem_inc(y_ready, 2)
                with dve.Fori(0, NU // 2) as n2:
                    for p in range(2):
                        n = n2 * 2 + p
                        dve.wait_ge(fg_ready, n + 1)
                        nc.vector.tensor_tensor(fg[:, p], fg[:, p], s_sb[:, bass.ds(n * S, S), :], ALU.mult).then_inc(prod, 1)
                        dve.wait_ge(prod, n + 1)
                        dve.wait_ge(x_in[p], n2 * 16 + 16)
                        dve.wait_ge(y_out[p], n2 * 16 + 16)
                        nc.vector.tensor_tensor(y[:, p], fg[:, p], xf[:, p], ALU.add).then_inc(y_ready, 1)


def kernel(**inputs):
    import numpy as np
    import concourse.bacc as bacc
    from concourse.bass_utils import run_bass_kernel_spmd

    a = {k: np.asarray(v) for k, v in inputs.items()}
    x = a["L0_attn_x"]
    B, L, _ = x.shape
    f = x.dtype

    def zeros(*shape):
        return np.zeros(shape, f)

    def by_chunk(w):
        return np.ascontiguousarray(w.reshape(KC, P, -1).transpose(1, 0, 2).reshape(P, -1))

    wproj = by_chunk(np.concatenate([a["L0_attn_Wk"], a["L0_attn_Wv"], a["L0_attn_Wu"], a["L0_ffn_sgate_w"].T,
                                     a["L0_ffn_gate_w"].T, zeros(H, 1), a["L0_attn_Wq"]], 1))
    wo = by_chunk(a["L0_attn_Wo"])
    sgu = a["L0_ffn_shared_gate_up_w"].reshape(2, SHARED, I, H).transpose(1, 0, 2, 3)
    gu = np.concatenate([a["L0_ffn_w13"].reshape(E, 2, I, H), sgu], 0)
    dn = np.concatenate([a["L0_ffn_w2"], a["L0_ffn_shared_down_w"].reshape(H, SHARED, I).transpose(1, 0, 2)], 0)
    guT = gu.transpose(0, 3, 1, 2)
    pad = zeros(NE, H, P // 2 - IR)
    up = np.concatenate([guT[:, :, 0, :P], guT[:, :, 0, P:], pad, guT[:, :, 1, P:], pad, guT[:, :, 1, :P]], 2)
    up = up.reshape(NE, KC, P, NUP).transpose(0, 2, 1, 3).reshape(NE, P, CD)
    dT = dn.transpose(0, 2, 1)
    rest = np.concatenate([dT[:, P:], zeros(NE, P // 2 - IR, H)], 1)
    wffn = np.ascontiguousarray(np.concatenate([up, dT[:, :P], np.concatenate([rest, rest], 1)], 2))
    head = np.arange(P) // HEAD
    consts = np.concatenate([np.eye(P), (head[:, None] == head[None, :]) / float(HEAD)], 1).astype(np.float32)
    xp = np.concatenate([x.reshape(B * L, H), zeros(2 * T, H)], 0)

    nc = bacc.Bacc("TRN2", target_bir_lowering=False, num_devices=1)
    arrays = {"x": xp, "wproj": wproj, "wo": wo, "wffn": wffn, "consts": consts}
    args = [nc.dram_tensor(n, v.shape, mybir.dt.from_np(v.dtype), kind="ExternalInput").ap() for n, v in arrays.items()]
    out = nc.dram_tensor("out", (B * L, H), F32, kind="ExternalOutput").ap()
    build(nc, *args, out)
    r = run_bass_kernel_spmd(nc, [arrays], core_ids=[0])
    return r.results[0]["out"].reshape(B, L, H)
```

```python
from contextlib import ExitStack

import concourse.bass as bass
from concourse import mybir

ALU = mybir.AluOpType
ACT = mybir.ActivationFunctionType
AX = mybir.AxisListType
F32 = mybir.dt.float32
R32 = mybir.dt.float32r
I32 = mybir.dt.int32

P = 128
HALF = P // 2
H = 256
KC = H // P
T = 256
S = T // P
HEAD = 16
E = 16
I = 176
SHARED = 4
NE = E + SHARED
IR = I - P
EPS = 1e-5
TOPK = 4
NONE = -3.0e38
MAGIC = float(0x5F3759DF)

CK, CV, CU, CG, CQ = 0, 256, 512, 768, 786
NG = CQ - CG
NPROJ = CQ + 256
NUP = 3 * P
CD = KC * NUP
NW = CD + 2 * H
NTOKENS = 4096
MAXTILE = NTOKENS * TOPK // T + E
NTILE = MAXTILE + 4
KI, KM, KL, KE, KR = 0, P, 2 * P, 3 * P, 3 * P + E
NCONST = KR + NTILE


def build(nc, x, wproj, wo, wffn, consts, out):
    NT = out.shape[0] // P
    NU = NT // S
    NB = 4
    UB = NU // NB
    TB = UB * S
    CAP = NU * T + T

    with ExitStack() as top:
        def psum(name, ctx):
            return ctx.enter_context(nc.psum_tensor(name, [P, 512], F32))

        def sem(name, ctx):
            return ctx.enter_context(nc.semaphore(name))

        def sb(name, shape, dt, ctx):
            return ctx.enter_context(nc.sbuf_tensor(name, shape, dt))

        xg = nc.dram_tensor("xg", (E * CAP, H), F32, kind="Internal").ap()
        yg = nc.dram_tensor("yg", (MAXTILE * T, H), F32, kind="Internal").ap()
        xnd = nc.dram_tensor("xnd", (NU * T, H), F32, kind="Internal").ap()

        xT_hi = sb("xT_hi", [P, KC, NU * T], R32, top)
        xT_lo = sb("xT_lo", [P, KC, NU * T], R32, top)
        s_sb = sb("s_sb", [P, NT, H], F32, top)
        ident = sb("ident", [P, P], F32, top)
        route = {
            "logit": sb("logit", [P, NT, 1 + E], F32, top),
            "slot": sb("slot", [P, NT, E], F32, top),
            "slot4": sb("slot4", [P, NT, TOPK], F32, top),
            "shift": sb("shift", [P, E], F32, top),
            "count": sb("count", [P, E], F32, top),
            "count_i": sb("count_i", [P, E], I32, top),
            "first": sb("first", [P, E + 1], I32, top),
            "tile_row": sb("tile_row", [P, NTILE], I32, top),
        }

        x_v = x.rearrange("(n s p) h -> n p s h", s=S, p=P)
        out_v = out.rearrange("(n s p) h -> n p s h", s=S, p=P)

        attention(nc, sb, psum, sem, x_v, wproj, wo, consts, xnd, xg, xT_hi, xT_lo, s_sb, route, ident, NT, NB, UB, TB, CAP)
        with ExitStack() as mid:
            wsh_hi = sb("wsh_hi", [P, SHARED, NW], R32, mid)
            wsh_lo = sb("wsh_lo", [P, SHARED, NW], R32, mid)
            routed_experts(nc, sb, psum, sem, wffn, consts, xg, yg, route, wsh_hi, wsh_lo, ident, CAP)
            shared_and_finish(nc, sb, psum, sem, wsh_hi, wsh_lo, x_v, yg, xT_hi, xT_lo, s_sb, route, out_v, NT, NU)


def rsqrt_steps(nc, link, v, vh, i32, y, t):
    link(nc.vector.tensor_scalar(i32, v.bitcast(I32), 1, None, ALU.logical_shift_right))
    nc.vector.tensor_scalar(vh, v, -0.5, None, ALU.mult)
    link(nc.vector.tensor_scalar(y.bitcast(I32), i32, -1.0, MAGIC, ALU.mult, ALU.add))
    for _ in range(4):
        link(nc.vector.tensor_tensor(t, vh, y, ALU.mult))
        link(nc.vector.tensor_tensor(t, t, y, ALU.mult))
        link(nc.vector.scalar_tensor_tensor(out=y, in0=t, scalar=1.5, in1=y, op0=ALU.add, op1=ALU.mult))


RSQRT_LINKS = 14


def attention(nc, sb, psum, sem, x_v, wproj, wo, consts, xnd, xg, xT_hi, xT_lo, s_sb, route, ident, NT, NB, UB, TB, CAP):
    DEAL = 16 * TOPK * TB
    with ExitStack() as ctx:
        mask = sb("mask", [P, P], F32, ctx)
        wp_raw = sb("wp_raw", [P, KC * NPROJ], F32, ctx)
        wp_hi = sb("wp_hi", [P, KC, NPROJ], R32, ctx)
        wp_lo = sb("wp_lo", [P, KC, NPROJ], R32, ctx)
        wo_raw = sb("wo_raw", [P, KC * H], F32, ctx)
        wo_hi = sb("wo_hi", [P, KC, H], R32, ctx)
        wo_lo = sb("wo_lo", [P, KC, H], R32, ctx)
        xin = sb("xin", [P, 2, S, H], F32, ctx)
        xn = sb("xn", [P, 2, S, H], F32, ctx)
        xs_hi = sb("xs_hi", [P, 2, KC, T], R32, ctx)
        xs_lo = sb("xs_lo", [P, 2, KC, T], R32, ctx)
        stats = sb("stats", [P, S, 6], F32, ctx)
        mv = sb("mv", [P, S, 2], F32, ctx)
        var = sb("var", [P, S], F32, ctx)
        varh = sb("varh", [P, S], F32, ctx)
        vari = sb("vari", [P, S], I32, ctx)
        rstd = sb("rstd", [P, S], F32, ctx)
        vart = sb("vart", [P, S], F32, ctx)
        k_hi = sb("k_hi", [P, S, H], R32, ctx)
        k_lo = sb("k_lo", [P, S, H], R32, ctx)
        v_hi = sb("v_hi", [P, S, H], R32, ctx)
        v_lo = sb("v_lo", [P, S, H], R32, ctx)
        q_hi = sb("q_hi", [P, KC, UB * T], R32, ctx)
        q_lo = sb("q_lo", [P, KC, UB * T], R32, ctx)
        kvm = sb("kvm", [P, KC, P], F32, ctx)
        kv_hi = sb("kv_hi", [P, KC, P], R32, ctx)
        kv_lo = sb("kv_lo", [P, KC, P], R32, ctx)
        u_sb = sb("u_sb", [P, TB, H], F32, ctx)
        sq = sb("sq", [P, 2, H], F32, ctx)
        ms = sb("ms", [P, TB * HEAD], F32, ctx)
        msh = sb("msh", [P, TB * HEAD], F32, ctx)
        msi = sb("msi", [P, TB * HEAD], I32, ctx)
        mst = sb("mst", [P, TB * HEAD], F32, ctx)
        rn = sb("rn", [P, TB * HEAD], F32, ctx)
        at = sb("at", [P, 2, H], F32, ctx)
        aT_hi = sb("aT_hi", [P, 2, KC, P], R32, ctx)
        aT_lo = sb("aT_lo", [P, 2, KC, P], R32, ctx)
        lg = sb("lg", [P, TB, 25], F32, ctx)
        top8 = sb("top8", [P, TB, 8], F32, ctx)
        rp = sb("rp", [P, TB, 24], F32, ctx)
        tri = sb("tri", [P, P], F32, ctx)
        ones = sb("ones", [P, P], F32, ctx)
        ebase = sb("ebase", [P, E], F32, ctx)
        chosen = sb("chosen", [P, TB, E], F32, ctx)
        before = sb("before", [P, TB + 1, E], F32, ctx)
        total = sb("total", [P, TB, E], F32, ctx)
        slot8 = sb("slot8", [P, TB, 8], F32, ctx)
        row_b = sb("row_b", [P, TB, TOPK], I32, ctx)
        zero = sb("zero", [P, S, H], F32, ctx)
        xrow = wp_raw[:, 0:TB * H].rearrange("p (t h) -> p t h", t=TB)

        psX = psum("psX", ctx)
        psKV = [psum(f"psKV{i}", ctx) for i in range(2)]
        psUG = [psum(f"psUG{i}", ctx) for i in range(2)]
        psQ = psum("psQ", ctx)
        psA = [psum(f"psA{i}", ctx) for i in range(2)]
        psT = [psX, psQ]

        s_w = sem("a_w", ctx)
        w_hi_done = sem("a_w_hi", ctx)
        w_done = sem("a_w_done", ctx)
        x_in = [sem(f"a_x_in{i}", ctx) for i in range(2)]
        x_copied = [sem(f"a_x_copied{i}", ctx) for i in range(2)]
        xn_ready = sem("a_xn_ready", ctx)
        xT_ps = sem("a_xT_ps", ctx)
        xh_ready = sem("a_xh_ready", ctx)
        xs_ready = sem("a_xs_ready", ctx)
        kv_ps = sem("a_kv_ps", ctx)
        kvh_ready = sem("a_kvh_ready", ctx)
        kvl_ready = sem("a_kvl_ready", ctx)
        ug_ps = sem("a_ug_ps", ctx)
        u_ready = sem("a_u_ready", ctx)
        q_ps = sem("a_q_ps", ctx)
        qh_ready = sem("a_qh_ready", ctx)
        unit_out = sem("a_unit_out", ctx)
        kva_ps = sem("a_kva_ps", ctx)
        kvb_ready = sem("a_kvb_ready", ctx)
        o_ps = sem("a_o_ps", ctx)
        sq_ready = sem("a_sq_ready", ctx)
        p_done = sem("a_p_done", ctx)
        at_ready = sem("a_at_ready", ctx)
        aT_ps = sem("a_aT_ps", ctx)
        ah_ready = sem("a_ah_ready", ctx)
        as_ready = sem("a_as_ready", ctx)
        s_ps = sem("a_s_ps", ctx)
        s_done = sem("a_s_done", ctx)
        xn_stored = [sem(f"a_xn_stored{i}", ctx) for i in range(2)]
        row_in = sem("a_row_in", ctx)
        dealt = sem("a_dealt", ctx)
        chosen_ready = sem("a_chosen", ctx)
        rank_ps = sem("a_rank_ps", ctx)
        rank_read = sem("a_rank_read", ctx)
        rows_ready = sem("a_rows_ready", ctx)
        rows_free = sem("a_rows_free", ctx)
        consts_set = sem("a_consts_set", ctx)
        counts_ready = sem("a_counts_ready", ctx)
        tails = sem("a_tails", ctx)
        dve_own = sem("a_dve_own", ctx)
        dve_passed = sem("a_dve_passed", ctx)
        pool_passed = sem("a_pool_passed", ctx)
        sp_passed = sem("a_sp_passed", ctx)

        with nc.Block() as block:

            @block.sync
            def _(sp):
                for p in range(2):
                    sp.sem_inc(x_copied[p], 16)
                sp.dma_start(ident[:, :], consts[:, KI:KI + P]).then_inc(s_w, 16)
                sp.dma_start(xin[:, 0], x_v[0]).then_inc(x_in[0], 16)
                sp.dma_start(wp_raw[:, :], wproj).then_inc(s_w, 16)
                sp.dma_start(xin[:, 1], x_v[1]).then_inc(x_in[1], 16)
                sp.dma_start(mask[:, :], consts[:, KM:KM + P]).then_inc(s_w, 16)
                sp.dma_start(wo_raw[:, :], wo).then_inc(s_w, 16)
                sp.dma_start(tri[:, :], consts[:, KL:KL + P]).then_inc(s_w, 16)
                sp.dma_start(ebase[:, :], consts[:, KE:KE + E]).then_inc(s_w, 16)
                sp.sem_inc(rows_free, 1)
                for p in range(2):
                    sp.sem_inc(xn_stored[p], 16)
                sp.wait_ge(w_done, 1)
                with sp.Fori(0, NB) as b:
                    for u in range(UB):
                        n, p = b * UB + u, u % 2
                        sp.wait_ge(xn_ready, n + 1)
                        sp.dma_start(xnd[bass.ds(n * T, T), :].rearrange("(s p) h -> p s h", p=P), xn[:, p]).then_inc(xn_stored[p], 16)
                        sp.dma_start(xin[:, p], x_v[bass.ds(n + 2, 1)].rearrange("o p s h -> p (o s) h")).then_inc(x_in[p], 16)
                        sp.wait_ge(xs_ready, n + 1)
                        sp.dma_start(f32(xT_hi[:, :, bass.ds(n * T, T)]), f32(xs_hi[:, p])).then_inc(x_copied[p], 16)
                        sp.dma_start(f32(xT_lo[:, :, bass.ds(n * T, T)]), f32(xs_lo[:, p])).then_inc(x_copied[p], 16)
                    for p in range(2):
                        sp.wait_ge(xn_stored[p], b * (16 * UB // 2) + 16 * UB // 2 + 16)
                        sp.sem_inc(sp_passed, 1)
                    sp.wait_ge(rows_free, b + 1)
                    sp.sem_inc(sp_passed, 1)
                    sp.dma_start(xrow, xnd[bass.ds(b * (TB * P), TB * P), :].rearrange("(t p) h -> p t h", p=P)).then_inc(row_in, 16)
                sp.wait_ge(counts_ready, 1)
                sp.wait_ge(rows_free, NB + 1)
                with sp.Fori(0, E) as e:
                    n_e = sp.value_load(route["count_i"][0:1, bass.ds(e, 1)], min_val=0, max_val=NTOKENS)
                    sp.dma_start(xg[bass.ds(e * CAP + n_e, T), :].rearrange("(s p) h -> p s h", p=P), zero[:, :, :]).then_inc(tails, 16)
                sp.wait_ge(tails, 16 * E)
                for p in range(2):
                    sp.wait_ge(x_copied[p], 32 * (NB * UB // 2) + 16)
                    sp.wait_ge(x_in[p], 16 * (NB * UB // 2 + 1))

            @block.gpsimd
            def _(pool):
                nc.gpsimd.memset(zero[:, :, :], 0.0)
                nc.gpsimd.memset(ones[:, :], 1.0).then_inc(consts_set, 1)
                with pool.Fori(0, NB) as b:
                    pool.wait_ge(rows_ready, b + 1)
                    pool.wait_ge(row_in, b * 16 + 16)
                    pool.sem_inc(pool_passed, 1)
                    for t in range(TB):
                        for k in range(TOPK):
                            nc.gpsimd.indirect_dma_start(
                                xg, bass.IndirectOffsetOnAxis(ap=row_b[:, t, k:k + 1].bitcast(mybir.dt.uint32), axis=0),
                                xrow[:, t, :], None).then_inc(dealt, 16)
                    pool.wait_ge(dealt, b * DEAL + DEAL)
                    pool.sem_inc(rows_free, 1)

            @block.scalar
            def _(act):
                nc.scalar.sem_inc(s_done, 1)
                act.preload_act_table(ACT.Silu)
                act.wait_ge(s_w, 96)
                nc.scalar.copy(wp_hi[:, :, :].rearrange("p k n -> p (k n)"), wp_raw[:, :])
                nc.scalar.copy(wo_hi[:, :, :].rearrange("p k n -> p (k n)"), wo_raw[:, :]).then_inc(w_hi_done, 1)
                act.wait_ge(xT_ps, 1)
                nc.scalar.copy(xs_hi[:, 0].rearrange("p k t -> p (k t)"), psX[:, :]).then_inc(xh_ready, 1)
                with act.Fori(0, NB) as b:
                    for u in range(UB):
                        n, p = b * UB + u, u % 2
                        for s in range(S):
                            act.wait_ge(kv_ps, n * S + s + 1)
                            nc.scalar.activation(k_hi[:, s], psKV[s][:, 0:H], ACT.Relu)
                            nc.scalar.copy(v_hi[:, s], psKV[s][:, H:2 * H]).then_inc(kvh_ready, 1)
                        act.wait_ge(xT_ps, n + 2)
                        act.wait_ge(x_copied[1 - p], b * (32 * UB // 2) + 32 * ((u + 1) // 2) + 16)
                        nc.scalar.copy(xs_hi[:, 1 - p].rearrange("p k t -> p (k t)"), psX[:, :]).then_inc(xh_ready, 1)
                        for s in range(S):
                            act.wait_ge(ug_ps, n * S + s + 1)
                            nc.scalar.activation(u_sb[:, u * S + s, :], psUG[s][:, 0:H], ACT.Silu).then_inc(u_ready, 1)
                        act.wait_ge(q_ps, n + 1)
                        nc.scalar.activation(q_hi[:, :, u * T:(u + 1) * T],
                                             psQ[:, :].rearrange("p (k t) -> p k t", k=KC), ACT.Relu).then_inc(qh_ready, 1)
                    for t in range(TB):
                        act.wait_ge(o_ps, b * TB + t + 1)
                        nc.scalar.activation(sq[:, t % 2], psKV[t % 2][:, 0:H], ACT.Square).then_inc(sq_ready, 1)

                    def head_out(t):
                        act.wait_ge(s_ps, b * TB + t + 1)
                        nc.scalar.copy(s_sb[:, bass.ds(b * TB + t, 1), :].rearrange("p o h -> p (o h)"),
                                       psUG[t % 2][:, 0:H]).then_inc(s_done, 1)

                    for t in range(TB):
                        act.wait_ge(aT_ps, b * TB + t + 1)
                        nc.scalar.copy(aT_hi[:, t % 2].rearrange("p k t -> p (k t)"), psT[t % 2][:, 0:H]).then_inc(ah_ready, 1)
                        if t:
                            head_out(t - 1)
                    head_out(TB - 1)

            @block.vector
            def _(dve):
                count = [0, 0]

                def link(ins):
                    ins.then_inc(dve_own, 1)
                    count[1] += 1
                    dve.wait_ge(dve_own, count[0] + count[1])

                def normalise(m_in, p, stored=None):
                    dve.wait_ge(x_in[p], m_in)
                    for s in range(S):
                        last = nc.vector.bn_stats(stats[:, s, :], xin[:, p, s, :])
                    link(last)
                    dve.sem_inc(dve_passed, 1)
                    for s in range(S):
                        last = nc.vector.bn_aggr(mv[:, s, :], stats[:, s, :])
                    link(last)
                    link(nc.vector.tensor_scalar(var[:, :], mv[:, :, 1], EPS, None, ALU.add))
                    rsqrt_steps(nc, link, var[:, :], varh[:, :], vari[:, :], rstd[:, :], vart[:, :])
                    if stored is not None:
                        dve.wait_ge(xn_stored[p], stored)
                    for s in range(S):
                        last = nc.vector.tensor_scalar(xn[:, p, s, :], xin[:, p, s, :], mv[:, s, 0:1],
                                                       rstd[:, s:s + 1], ALU.subtract, ALU.mult)
                    last.then_inc(xn_ready, 1)

                def split_x(p):
                    nc.vector.tensor_tensor(xs_lo[:, p].rearrange("p k t -> p (k t)"), psX[:, :],
                                            f32(xs_hi[:, p].rearrange("p k t -> p (k t)")), ALU.subtract).then_inc(xs_ready, 1)

                nc.vector.sem_inc(unit_out, 1)
                nc.vector.memset(lg[:, :, :], NONE)
                nc.vector.memset(before[:, 0, :], 0.0)
                normalise(16, 0)
                dve.wait_ge(w_hi_done, 1)
                nc.vector.tensor_tensor(wp_lo[:, :, :].rearrange("p k n -> p (k n)"), wp_raw[:, :],
                                        f32(wp_hi[:, :, :].rearrange("p k n -> p (k n)")), ALU.subtract)
                nc.vector.tensor_tensor(wo_lo[:, :, :].rearrange("p k n -> p (k n)"), wo_raw[:, :],
                                        f32(wo_hi[:, :, :].rearrange("p k n -> p (k n)")), ALU.subtract).then_inc(w_done, 1)
                dve.wait_ge(xh_ready, 1)
                split_x(0)
                normalise(16, 1)
                LINKS0 = count[1]
                links_per_seq = UB * (3 + RSQRT_LINKS) + 2 + (1 + RSQRT_LINKS) + 3 + (1 + TB + 3) + 3
                with dve.Fori(0, NB) as b:
                    count[0], count[1] = LINKS0 + b * links_per_seq, 0
                    for u in range(UB):
                        n, p = b * UB + u, u % 2
                        for s in range(S):
                            dve.wait_ge(kvh_ready, n * S + s + 1)
                            nc.vector.scalar_tensor_tensor(out=k_lo[:, s], in0=psKV[s][:, 0:H], scalar=0.0,
                                                           in1=f32(k_hi[:, s]), op0=ALU.max, op1=ALU.subtract)
                            nc.vector.tensor_tensor(v_lo[:, s], psKV[s][:, H:2 * H], f32(v_hi[:, s]),
                                                    ALU.subtract).then_inc(kvl_ready, 1)
                        dve.wait_ge(xh_ready, n + 2)
                        split_x(1 - p)
                        for s in range(S):
                            dve.wait_ge(u_ready, n * S + s + 1)
                            nc.vector.tensor_copy(lg[:, u * S + s, 0:17], psUG[s][:, H:H + 17])
                        dve.wait_ge(qh_ready, n + 1)
                        nc.vector.scalar_tensor_tensor(out=q_lo[:, :, u * T:(u + 1) * T],
                                                       in0=psQ[:, :].rearrange("p (k t) -> p k t", k=KC), scalar=0.0,
                                                       in1=f32(q_hi[:, :, u * T:(u + 1) * T]),
                                                       op0=ALU.max, op1=ALU.subtract).then_inc(unit_out, 1)
                        normalise(b * (16 * UB // 2) + 16 * (u // 2 + 2), p, b * (16 * UB // 2) + 16 * (u // 2 + 1) + 16)
                    dve.wait_ge(kva_ps, b + 1)
                    for c in range(KC):
                        last = nc.vector.tensor_tensor(kvm[:, c], psA[c][:, 0:P], mask[:, :], ALU.mult)
                    link(last)
                    link(nc.vector.tensor_copy(kv_hi[:, :, :], kvm[:, :, :]))
                    nc.vector.tensor_tensor(kv_lo[:, :, :], kvm[:, :, :], f32(kv_hi[:, :, :]), ALU.subtract).then_inc(kvb_ready, 1)
                    for t in range(TB):
                        last = nc.vector.max(top8[:, t, :], lg[:, t, 1:17])
                    link(last)
                    link(nc.vector.memset(top8[:, :, 4:8], NONE))
                    dve.sem_inc(dve_passed, 1)
                    for t in range(TB):
                        last = nc.vector.match_replace(rp[:, t, :], top8[:, t, :], lg[:, t, 1:25], NONE)
                    link(last)
                    nc.vector.tensor_copy(route["logit"][:, bass.ds(b * TB, TB), :], lg[:, :, 0:17])
                    nc.vector.tensor_tensor(chosen[:, :, :], rp[:, :, 0:E], lg[:, :, 1:17], ALU.not_equal).then_inc(chosen_ready, 1)
                    dve.wait_ge(rank_ps, b + 1)
                    link(nc.vector.tensor_copy(total[:, :, :], psQ[:, P:2 * P].rearrange("p (t e) -> p t e", e=E)))
                    for t in range(TB):
                        link(nc.vector.tensor_tensor(before[:, t + 1, :], before[:, t, :], total[:, t, :], ALU.add))
                    link(nc.vector.tensor_tensor(total[:, :, :], psQ[:, 0:P].rearrange("p (t e) -> p t e", e=E),
                                                 before[:, 0:TB, :], ALU.add))
                    link(nc.vector.tensor_tensor(total[:, :, :], total[:, :, :],
                                                 ebase[:, :].unsqueeze(1).broadcast_to([P, TB, E]), ALU.add))
                    link(nc.vector.tensor_tensor(total[:, :, :], total[:, :, :], chosen[:, :, :], ALU.mult))
                    nc.vector.tensor_copy(before[:, 0, :], before[:, TB, :])
                    for t in range(TB):
                        last = nc.vector.max(slot8[:, t, :], total[:, t, :])
                    link(last)
                    dve.wait_ge(rows_free, b + 1)
                    dve.sem_inc(dve_passed, 1)
                    link(nc.vector.tensor_scalar(row_b[:, :, :], slot8[:, :, 0:TOPK], 1.0, None, ALU.subtract))
                    nc.vector.tensor_copy(route["slot4"][:, bass.ds(b * TB, TB), :], slot8[:, :, 0:TOPK])
                    link(nc.vector.tensor_copy(route["slot"][:, bass.ds(b * TB, TB), :], total[:, :, :]))
                    dve.sem_inc(rows_ready, 1)
                    for t in range(TB):
                        dve.wait_ge(sq_ready, b * TB + t + 1)
                        last = nc.vector.tensor_reduce(ms[:, t * HEAD:(t + 1) * HEAD],
                                                       sq[:, t % 2].rearrange("p (h d) -> p h d", d=HEAD), AX.X, ALU.add)
                        nc.vector.tensor_tensor(u_sb[:, t, :], psKV[t % 2][:, 0:H], u_sb[:, t, :], ALU.mult).then_inc(p_done, 1)
                        if t == TB - 1:
                            dve.wait_ge(p_done, b * TB + TB)
                    link(nc.vector.tensor_scalar(ms[:, :], ms[:, :], 1.0 / HEAD, 1e-24, ALU.mult, ALU.max))
                    rsqrt_steps(nc, link, ms[:, :], msh[:, :], msi[:, :], rn[:, :], mst[:, :])

                    def split_a(t):
                        dve.wait_ge(ah_ready, b * TB + t + 1)
                        nc.vector.tensor_tensor(aT_lo[:, t % 2].rearrange("p k t -> p (k t)"), psT[t % 2][:, 0:H],
                                                f32(aT_hi[:, t % 2].rearrange("p k t -> p (k t)")),
                                                ALU.subtract).then_inc(as_ready, 1)

                    for t in range(TB):
                        if t >= 2:
                            dve.wait_ge(aT_ps, b * TB + t - 1)
                        nc.vector.tensor_tensor(
                            at[:, t % 2].rearrange("p (h d) -> p h d", d=HEAD),
                            u_sb[:, t, :].rearrange("p (h d) -> p h d", d=HEAD),
                            rn[:, t * HEAD:(t + 1) * HEAD].unsqueeze(2).broadcast_to([P, HEAD, HEAD]),
                            ALU.mult).then_inc(at_ready, 1)
                        if t:
                            split_a(t - 1)
                    split_a(TB - 1)
                    assert count[1] == links_per_seq, count[1]
                count[0], count[1] = LINKS0 + NB * links_per_seq, 0
                nc.vector.tensor_copy(route["count"][:, :], before[:, 0, :])
                nc.vector.tensor_copy(route["count_i"][:, :], before[:, 0, :]).then_inc(counts_ready, 1)

            @block.tensor
            def _(pe):
                def transpose_x(p):
                    for k in range(KC):
                        for s in range(S):
                            last = nc.tensor.transpose(psX[:, k * T + s * P:k * T + (s + 1) * P],
                                                       xn[:, p, s, k * P:(k + 1) * P], ident[:, :])
                    last.then_inc(xT_ps, 1)

                def products(out, lhs, rhs):
                    i = 0
                    for k in range(len(lhs)):
                        (ah, al), (bh, bl) = lhs[k], rhs[k]
                        for a, c in ((ah, bh), (ah, bl), (al, bh)):
                            last = nc.tensor.matmul(out, a, c, start=i == 0, stop=i == 3 * len(lhs) - 1)
                            i += 1
                    return last

                def wcols(k, a, n):
                    return wp_hi[:, k, a:a + n], wp_lo[:, k, a:a + n]

                pe.wait_ge(s_w, 96)
                pe.wait_ge(xn_ready, 1)
                transpose_x(0)
                pe.wait_ge(w_done, 1)
                with pe.Fori(0, NB) as b:
                    for u in range(UB):
                        n, p = b * UB + u, u % 2

                        def xcols(k, a, n):
                            return xs_hi[:, p, k, a:a + n], xs_lo[:, p, k, a:a + n]

                        pe.wait_ge(xs_ready, n + 1)
                        for s in range(S):
                            products(psKV[s][:, :], [xcols(k, s * P, P) for k in range(KC)],
                                     [wcols(k, CK, 2 * H) for k in range(KC)]).then_inc(kv_ps, 1)
                        pe.wait_ge(xn_ready, n + 2)
                        transpose_x(1 - p)
                        pe.wait_ge(unit_out, n + 1)
                        if u == 0:
                            pe.wait_ge(s_done, b * TB + 1)
                        for s in range(S):
                            for k in range(KC):
                                (xh, xl), (wh, wl) = xcols(k, s * P, P), wcols(k, CU, H + NG)
                                nc.tensor.matmul(psUG[s][:, 0:H + NG], xh, wh, start=k == 0, stop=False)
                                nc.tensor.matmul(psUG[s][:, 0:H + NG], xh, wl, start=False, stop=False)
                                nc.tensor.matmul(psUG[s][:, H:H + NG], xl, wl[:, H:H + NG], start=False, stop=False,
                                                 skip_group_check=True)
                                last = nc.tensor.matmul(psUG[s][:, 0:H + NG], xl, wh, start=False, stop=k == KC - 1)
                            last.then_inc(ug_ps, 1)
                        for c in range(KC):
                            last = products(psQ[:, c * T:(c + 1) * T], [wcols(k, CQ + c * P, P) for k in range(KC)],
                                            [xcols(k, 0, T) for k in range(KC)])
                        last.then_inc(q_ps, 1)
                        pe.wait_ge(kvl_ready, n * S + S)
                        for s in range(S):
                            for c in range(KC):
                                kk = slice(c * P, (c + 1) * P)
                                for i, (a, v) in enumerate(((k_hi, v_hi), (k_hi, v_lo), (k_lo, v_hi))):
                                    last = nc.tensor.matmul(psA[c][:, 0:P], a[:, s, kk], v[:, s, kk],
                                                            start=u == 0 and s == 0 and i == 0,
                                                            stop=u == UB - 1 and s == S - 1 and i == 2)
                    last.then_inc(kva_ps, 1)
                    pe.wait_ge(chosen_ready, b + 1)
                    pe.wait_ge(consts_set, 1)
                    nc.tensor.matmul(psQ[:, 0:P], tri[:, :], chosen[:, :, :].rearrange("p t e -> p (t e)"), start=True, stop=True)
                    nc.tensor.matmul(psQ[:, P:2 * P], ones[:, :], chosen[:, :, :].rearrange("p t e -> p (t e)"), start=True,
                                     stop=True).then_inc(rank_ps, 1)
                    pe.wait_ge(kvb_ready, b + 1)
                    for t in range(TB):
                        if t >= 2:
                            pe.wait_ge(p_done, b * TB + t - 1)
                        for c in range(KC):
                            last = products(psKV[t % 2][:, c * P:(c + 1) * P],
                                            [(q_hi[:, c, t * P:(t + 1) * P], q_lo[:, c, t * P:(t + 1) * P])],
                                            [(kv_hi[:, c], kv_lo[:, c])])
                        last.then_inc(o_ps, 1)

                    def head_out(t):
                        pe.wait_ge(as_ready, b * TB + t + 1)
                        if t >= 2:
                            pe.wait_ge(s_done, b * TB + t)
                        products(psUG[t % 2][:, 0:H], [(aT_hi[:, t % 2, k], aT_lo[:, t % 2, k]) for k in range(KC)],
                                 [(wo_hi[:, k], wo_lo[:, k]) for k in range(KC)]).then_inc(s_ps, 1)

                    for t in range(TB):
                        pe.wait_ge(at_ready, b * TB + t + 1)
                        for k in range(KC):
                            last = nc.tensor.transpose(psT[t % 2][:, k * P:(k + 1) * P], at[:, t % 2, k * P:(k + 1) * P],
                                                       ident[:, :])
                        last.then_inc(aT_ps, 1)
                        if t:
                            head_out(t - 1)
                    head_out(TB - 1)


def f32(ap):
    return ap.bitcast(F32)


class Ffn:

    def __init__(self, tag, sb, psum, sem, ctx):
        self.sg0 = sb(tag + "sg0", [P, T], F32, ctx)
        self.sgm = sb(tag + "sgm", [P, T], F32, ctx)
        self.h0 = sb(tag + "h0", [P, T], F32, ctx)
        self.hm = sb(tag + "hm", [P, T], F32, ctx)
        self.h0_hi = sb(tag + "h0_hi", [P, T], R32, ctx)
        self.h0_lo = sb(tag + "h0_lo", [P, T], R32, ctx)
        self.hm_s = sb(tag + "hm_s", [P, T], R32, ctx)
        self.psG = psum(tag + "psG", ctx)
        self.psM = psum(tag + "psM", ctx)
        self.psU = psum(tag + "psU", ctx)
        self.up_ps = sem(tag + "up_ps", ctx)
        self.sg_ready = sem(tag + "sg_ready", ctx)
        self.h_done = sem(tag + "h_done", ctx)
        self.hh_ready = sem(tag + "hh_ready", ctx)
        self.hl_ready = sem(tag + "hl_ready", ctx)
        self.down_ps = sem(tag + "down_ps", ctx)

    def start_vector(self, nc):
        nc.vector.sem_inc(self.h_done, 1)
        nc.vector.sem_inc(self.hl_ready, 1)

    def start_tensor(self, pe):
        pe.sem_inc(self.down_ps, 1)

    def up(self, nc, pe, q, w_hi, w_lo, x_hi, x_lo, between=None):
        pe.wait_ge(self.h_done, q + 1)
        for c, bank in enumerate((self.psG, self.psM, self.psU)):
            i = 0
            for k in range(KC):
                cols = slice(k * NUP + c * P, k * NUP + (c + 1) * P)
                for w, xx in ((w_hi, x_hi), (w_hi, x_lo), (w_lo, x_hi)):
                    last = nc.tensor.matmul(bank[:, 0:T], w[:, cols], xx(k), start=i == 0, stop=i == 5)
                    i += 1
            last.then_inc(self.up_ps, 1)
            if c == 0 and between:
                between()

    def down(self, nc, pe, q, w_hi, w_lo, out, first=True, last_of_sum=True):
        pe.wait_ge(self.hl_ready, q + 2)
        d0, d1 = slice(CD, CD + H), slice(CD + H, NW)
        ops = ((self.h0_hi, w_hi, d0), (self.h0_hi, w_lo, d0), (self.h0_lo, w_hi, d0),
               (self.hm_s, w_hi, d1), (self.hm_s, w_lo, d1))
        for s in range(S):
            for i, (h, w, d) in enumerate(ops):
                last = nc.tensor.matmul(out[s], h[:, s * P:(s + 1) * P], w[:, d], start=first and i == 0,
                                        stop=last_of_sum and i == len(ops) - 1)
        last.then_inc(self.down_ps, 1)

    def gate0(self, nc, act, q):
        act.wait_ge(self.up_ps, q * 3 + 1)
        nc.scalar.activation(self.sg0[:, :], self.psG[:, 0:T], ACT.Silu).then_inc(self.sg_ready, 1)

    def gate_rest(self, nc, act, q):
        act.wait_ge(self.up_ps, q * 3 + 2)
        nc.scalar.activation(self.sgm[0:HALF, :], self.psM[0:HALF, 0:T], ACT.Silu).then_inc(self.sg_ready, 1)

    def high(self, nc, act, q):
        act.wait_ge(self.h_done, q + 2)
        act.wait_ge(self.down_ps, q + 1)
        nc.scalar.copy(self.h0_hi[:, :], self.h0[:, :])
        nc.scalar.copy(self.hm_s[0:HALF, :], self.hm[0:HALF, :]).then_inc(self.hh_ready, 1)

    def hidden(self, nc, dve, q):
        dve.wait_ge(self.up_ps, q * 3 + 3)
        dve.wait_ge(self.sg_ready, q * 2 + 2)
        dve.wait_ge(self.hl_ready, q + 1)
        nc.vector.tensor_tensor(self.h0[:, :], self.psU[:, 0:T], self.sg0[:, :], ALU.mult)
        nc.vector.tensor_tensor(self.hm[0:HALF, :], self.psM[HALF:P, 0:T], self.sgm[0:HALF, :],
                                ALU.mult).then_inc(self.h_done, 1)

    def low(self, nc, dve, q):
        dve.wait_ge(self.hh_ready, q + 1)
        nc.vector.tensor_tensor(self.h0_lo[:, :], self.h0[:, :], f32(self.h0_hi[:, :]), ALU.subtract)
        nc.vector.tensor_tensor(self.hm_s[HALF:P, :], self.hm[0:HALF, :], f32(self.hm_s[0:HALF, :]),
                                ALU.subtract).then_inc(self.hl_ready, 1)


def tile_tables(nc, dve, link, consts_sb, route, tmp):
    tile_i, tiles, firstf, step, cmp, row = (tmp[k] for k in ("tile_i", "tiles", "firstf", "step", "cmp", "row"))
    start = consts_sb[:, :]
    link(nc.vector.tensor_scalar(tile_i[:, :], route["count"][:, :], T - 1.0, None, ALU.add))
    link(nc.vector.tensor_scalar(tile_i[:, :], tile_i[:, :], T.bit_length() - 1, None, ALU.logical_shift_right))
    link(nc.vector.tensor_scalar(tiles[:, :], tile_i[:, :], 1.0, None, ALU.max))
    link(nc.vector.memset(firstf[:, 0:1], 0.0))
    for e in range(E):
        link(nc.vector.tensor_tensor(firstf[:, e + 1:e + 2], firstf[:, e:e + 1], tiles[:, e:e + 1], ALU.add))
    link(nc.vector.tensor_copy(route["first"][:, :], firstf[:, :]))
    link(nc.vector.tensor_scalar(step[:, :], tiles[:, :], -float(T), float(tmp["cap"]), ALU.mult, ALU.add))
    link(nc.vector.tensor_scalar(firstf[:, :], firstf[:, :], float(T), None, ALU.mult))
    link(nc.vector.tensor_tensor(cmp[:, :, :], start.unsqueeze(2).broadcast_to([P, NTILE, E]),
                                 firstf[:, 1:E + 1].unsqueeze(1).broadcast_to([P, NTILE, E]), ALU.is_ge))
    link(nc.vector.tensor_tensor(cmp[:, :, :], cmp[:, :, :], step[:, :].unsqueeze(1).broadcast_to([P, NTILE, E]), ALU.mult))
    link(nc.vector.tensor_reduce(row[:, :], cmp[:, :, :], AX.X, ALU.add))
    link(nc.vector.tensor_tensor(row[:, :], row[:, :], start, ALU.add))
    link(nc.vector.tensor_scalar(cmp[:, :, 0], start, firstf[:, E:E + 1], None, ALU.is_lt))
    return nc.vector.tensor_tensor(route["tile_row"][:, :], row[:, :], cmp[:, :, 0], ALU.mult)


def split_weights(nc, pool, raw, w_hi, w_lo, own, n, done):
    nc.gpsimd.tensor_copy(w_hi, raw).then_inc(own, 1)
    pool.wait_ge(own, n)
    nc.gpsimd.tensor_tensor(w_lo[:, 0:CD + H], raw[:, 0:CD + H], f32(w_hi[:, 0:CD + H]), ALU.subtract)
    nc.gpsimd.tensor_tensor(w_lo[0:HALF, CD + H:NW], raw[0:HALF, CD + H:NW], f32(w_hi[0:HALF, CD + H:NW]),
                            ALU.subtract).then_inc(done, 1)


def routed_experts(nc, sb, psum, sem, wffn, consts, xg, yg, route, wsh_hi, wsh_lo, ident, CAP):
    with ExitStack() as ctx:
        RING = 4
        w_raw = sb("w_raw", [P, 2, NW], F32, ctx)
        w_hi = sb("w_hi", [P, 2, NW], R32, ctx)
        w_lo = sb("w_lo", [P, 2, NW], R32, ctx)
        ring = sb("ring", [P, RING, S, H], F32, ctx)
        rows = sb("rows", [P, S, H], F32, ctx)
        x_hi = sb("x_hi", [P, KC, 2 * T], R32, ctx)
        x_lo = sb("x_lo", [P, KC, 2 * T], R32, ctx)
        y = sb("y", [P, 2, S * H], F32, ctx)
        zero = sb("e_zero", [P, S, H], F32, ctx)
        start = sb("start", [P, NTILE], F32, ctx)
        ebase = sb("e_ebase", [P, E], F32, ctx)
        tmp = {"tile_i": sb("tile_i", [P, E], I32, ctx), "tiles": sb("tiles", [P, E], F32, ctx),
               "firstf": sb("firstf", [P, E + 1], F32, ctx), "step": sb("step", [P, E], F32, ctx),
               "cmp": ring[:, :, :, :].rearrange("p r s h -> p (r s h)")[:, 0:NTILE * E].rearrange("p (g e) -> p g e", e=E),
               "row": sb("row", [P, NTILE], F32, ctx), "cap": CAP}
        ffn = Ffn("e_", sb, psum, sem, ctx)
        psX = psum("e_psX", ctx)
        psD = psum("e_psD", ctx)

        s_c = sem("e_consts", ctx)
        tables = sem("e_tables", ctx)
        w_in = [sem(f"e_w_in{i}", ctx) for i in range(2)]
        zeroed = sem("e_zeroed", ctx)
        wh_done = sem("e_wh_done", ctx)
        w_ready = sem("e_w_ready", ctx)
        landed = sem("e_landed", ctx)
        copied = sem("e_copied", ctx)
        xT_ps = sem("e_xT_ps", ctx)
        xh_ready = sem("e_xh_ready", ctx)
        xs_ready = sem("e_xs_ready", ctx)
        y_ready = sem("e_y_ready", ctx)
        stored = sem("e_stored", ctx)
        cleared = sem("e_cleared", ctx)
        own = sem("e_dve_own", ctx)
        passed = {k: sem(f"e_passed_{k}", ctx) for k in ("dve", "act", "pool", "sp")}

        def over_experts(body):
            body(0, 0, True)

            def pairs(eng):
                with eng.Fori(0, E // 2 - 1) as j:
                    for p in (1, 0):
                        body(j * 2 + 2 - p, p, False)
            return pairs

        def expert_tiles(eng, e, first_tile, next_tile):
            f = route["first"]
            g0 = eng.value_load(f[0:1, bass.ds(e, 1)], min_val=0, max_val=NTILE - 5)
            g1 = eng.value_load(f[0:1, bass.ds(e + 1, 1)], min_val=1, max_val=NTILE - 4)
            first_tile(g0)
            with eng.If(g1 > g0 + 1):
                with eng.Fori(g0 + 1, g1) as g:
                    next_tile(g)

        with nc.Block() as block:

            @block.sync
            def _(sp):
                sp.sem_inc(stored, 32)
                sp.dma_start(start[:, :], consts[:, KR:KR + NTILE]).then_inc(s_c, 16)
                sp.dma_start(ebase[:, :], consts[:, KE:KE + E]).then_inc(s_c, 16)
                sp.wait_ge(tables, 1)

                def load(g, slot):
                    row = sp.value_load(route["tile_row"][0:1, bass.ds(g, 1)], min_val=0, max_val=E * CAP - T)
                    sp.dma_start(ring[:, slot], xg[bass.ds(row, T), :].rearrange("(s p) h -> p s h", p=P)).then_inc(landed, 16)

                for g in range(RING):
                    load(g, g)
                    sp.wait_ge(landed, 16 * (g + 1))
                tiles = sp.value_load(route["first"][0:1, E:E + 1], min_val=1, max_val=NTILE - 4)
                with sp.Fori(0, tiles) as g:
                    sp.sem_inc(cleared, 16)
                    sp.wait_ge(copied, g + 1)
                    sp.sem_inc(passed["sp"], 1)
                    row = sp.value_load(route["tile_row"][0:1, bass.ds(g + RING, 1)], min_val=0, max_val=E * CAP - T)
                    sp.dma_start(ring[:, bass.ds(g % RING, 1)].rearrange("p o s h -> p (o s) h"),
                                 xg[bass.ds(row, T), :].rearrange("(s p) h -> p s h", p=P)).then_inc(landed, 16)
                    sp.wait_ge(landed, g * 16 + 16 * (RING + 1))
                    sp.sem_inc(passed["sp"], 1)
                    sp.wait_ge(y_ready, g + 2)
                    sp.sem_inc(passed["sp"], 1)
                    sp.wait_ge(stored, g * 16 + 32)
                    sp.dma_start(yg[bass.ds(g * T, T), :].rearrange("(s p) h -> p s h", p=P),
                                 y[:, bass.ds(g % 2, 1)].rearrange("p o (s h) -> p (o s) h", s=S)).then_inc(stored, 16)
                with sp.If(tiles < MAXTILE):
                    with sp.Fori(tiles, MAXTILE) as g:
                        sp.dma_start(yg[bass.ds(g * T, T), :].rearrange("(s p) h -> p s h", p=P), zero[:, :, :]).then_inc(cleared, 16)
                sp.wait_ge(cleared, MAXTILE * 16)
                sp.wait_ge(stored, tiles * 16 + 32)
                sp.sem_inc(passed["sp"], 1)

            @block.gpsimd
            def _(pool):
                for p in range(2):
                    pool.dma_start(w_raw[:, p], wffn[p]).then_inc(w_in[p], 16)
                nc.gpsimd.memset(f32(wsh_lo[HALF:P, :, CD + H:NW]), 0.0)
                nc.gpsimd.memset(f32(w_lo[HALF:P, :, CD + H:NW]), 0.0).then_inc(zeroed, 1)
                pool.wait_ge(zeroed, 1)
                for e in range(2):
                    pool.wait_ge(w_in[e], 16)
                    split_weights(nc, pool, w_raw[:, e], w_hi[:, e], w_lo[:, e], wh_done, e + 1, w_ready)
                    pool.wait_ge(w_ready, e + 1)
                    pool.dma_start(w_raw[:, e], wffn[e + 2]).then_inc(w_in[e], 16)
                pool.wait_ge(tables, 1)
                with pool.Fori(1, E // 2) as j:
                    for p in range(2):
                        e = j * 2 + p
                        g = pool.value_load(route["first"][0:1, bass.ds(e - 1, 1)], min_val=1, max_val=NTILE - 4)
                        pool.wait_ge(ffn.down_ps, g + 1)
                        pool.wait_ge(w_in[p], j * 16 + 16)
                        pool.sem_inc(passed["pool"], 1)
                        split_weights(nc, pool, w_raw[:, p], w_hi[:, p], w_lo[:, p], wh_done, e + 1, w_ready)
                        pool.wait_ge(w_ready, e + 1)
                        pool.sem_inc(passed["pool"], 1)
                        pool.dma_start(w_raw[:, p], wffn[bass.ds(e + 2, 1)].rearrange("o p n -> p (o n)")).then_inc(w_in[p], 16)
                for j in range(SHARED):
                    p = j % 2
                    pool.wait_ge(w_in[p], 16 * (E // 2 + j // 2 + 1))
                    split_weights(nc, pool, w_raw[:, p], wsh_hi[:, j], wsh_lo[:, j], wh_done, E + j + 1, w_ready)
                    if j < 2:
                        pool.wait_ge(w_ready, E + j + 1)
                        pool.dma_start(w_raw[:, p], wffn[E + j + 2]).then_inc(w_in[p], 16)

            @block.scalar
            def _(act):
                act.preload_act_table(ACT.Silu)
                act.wait_ge(tables, 1)

                def high_x(g):
                    act.wait_ge(xT_ps, g + 1)
                    act.sem_inc(passed["act"], 1)
                    nc.scalar.copy(x_hi[:, :, bass.ds((g % 2) * T, T)],
                                   psX[:, :].rearrange("p (k t) -> p k t", k=KC)).then_inc(xh_ready, 1)

                def result(g):
                    act.wait_ge(ffn.down_ps, g + 2)
                    act.wait_ge(stored, g * 16 + 16)
                    act.sem_inc(passed["act"], 1)
                    nc.scalar.copy(y[:, bass.ds(g % 2, 1), :].rearrange("p o n -> p (o n)"), psD[:, :]).then_inc(y_ready, 1)

                def tile(g, before=True):
                    ffn.gate0(nc, act, g)
                    high_x(g + 1)
                    ffn.gate_rest(nc, act, g)
                    ffn.high(nc, act, g)
                    if before:
                        result(g - 1)

                high_x(0)

                def expert(e, p, first):
                    expert_tiles(act, e, lambda g: tile(g, not first), tile)

                over_experts(expert)(act)
                expert(E - 1, 1, False)
                tiles = act.value_load(route["first"][0:1, E:E + 1], min_val=1, max_val=NTILE - 4)
                result(tiles - 1)

            @block.vector
            def _(dve):
                n_own = [0]

                def link(ins):
                    ins.then_inc(own, 1)
                    n_own[0] += 1
                    dve.wait_ge(own, n_own[0])

                dve.wait_ge(s_c, 32)
                nc.vector.memset(zero[:, :, :], 0.0)
                tile_tables(nc, dve, link, start, route, tmp).then_inc(tables, 1)
                dve.wait_ge(tables, 1)
                link(nc.vector.tensor_tensor(route["shift"][:, :], tmp["firstf"][:, 0:E], ebase[:, :], ALU.subtract))
                ffn.start_vector(nc)
                nc.vector.sem_inc(y_ready, 1)

                def copy_rows(g):
                    dve.wait_ge(landed, g * 16 + 16)
                    dve.wait_ge(xT_ps, g)
                    dve.sem_inc(passed["dve"], 1)
                    nc.vector.tensor_copy(rows[:, :, :], ring[:, bass.ds(g % RING, 1)].rearrange("p o s h -> p (o s) h")).then_inc(copied, 1)

                def low_x(g):
                    cols = bass.ds((g % 2) * T, T)
                    dve.wait_ge(xh_ready, g + 1)
                    nc.vector.tensor_tensor(x_lo[:, :, cols], psX[:, :].rearrange("p (k t) -> p k t", k=KC),
                                            f32(x_hi[:, :, cols]), ALU.subtract).then_inc(xs_ready, 1)

                def tile(g):
                    copy_rows(g + 1)
                    low_x(g + 1)
                    ffn.hidden(nc, dve, g)
                    ffn.low(nc, dve, g)

                dve.wait_ge(landed, 16)
                nc.vector.tensor_copy(rows[:, :, :], ring[:, 0]).then_inc(copied, 1)
                low_x(0)

                def expert(e, p, first):
                    expert_tiles(dve, e, tile, tile)

                over_experts(expert)(dve)
                expert(E - 1, 1, False)

            @block.tensor
            def _(pe):
                ffn.start_tensor(pe)
                pe.wait_ge(tables, 1)

                def transpose(g):
                    pe.wait_ge(copied, g + 1)
                    for k in range(KC):
                        for s in range(S):
                            last = nc.tensor.transpose(psX[:, k * T + s * P:k * T + (s + 1) * P],
                                                       rows[:, s, k * P:(k + 1) * P], ident[:, :])
                    last.then_inc(xT_ps, 1)

                def up(g, p):
                    pe.wait_ge(xs_ready, g + 1)
                    cols = bass.ds((g % 2) * T, T)
                    ffn.up(nc, pe, g, w_hi[:, p], w_lo[:, p], lambda k: x_hi[:, k, cols], lambda k: x_lo[:, k, cols],
                           between=lambda: transpose(g + 1))

                def down(g, p):
                    pe.wait_ge(y_ready, g + 1)
                    ffn.down(nc, pe, g, w_hi[:, p], w_lo[:, p], [psD[:, s * H:(s + 1) * H] for s in range(S)])

                transpose(0)

                def expert(e, p, first):
                    def first_tile(g):
                        pe.wait_ge(w_ready, e + 1)
                        up(g, p)
                        if not first:
                            down(g - 1, 1 - p)

                    def next_tile(g):
                        up(g, p)
                        down(g - 1, p)

                    expert_tiles(pe, e, first_tile, next_tile)

                over_experts(expert)(pe)
                expert(E - 1, 1, False)
                tiles = pe.value_load(route["first"][0:1, E:E + 1], min_val=1, max_val=NTILE - 4)
                down(tiles - 1, 1)


def shared_and_finish(nc, sb, psum, sem, wsh_hi, wsh_lo, x_v, yg, xT_hi, xT_lo, s_sb, route, out_v, NT, NU):
    with ExitStack() as ctx:
        ex = sb("ex", [P, NT, E], F32, ctx)
        pick = sb("pick", [P, NT, E], F32, ctx)
        lmax = sb("lmax", [P, NT], F32, ctx)
        den = sb("den", [P, NT], F32, ctx)
        gate = sb("gate", [P, NT], F32, ctx)
        weight = sb("weight", [P, TOPK, NT], F32, ctx)
        row4 = sb("row4", [P, NT, TOPK], I32, ctx)
        row_u = sb("row_u", [P, 2, S * TOPK], I32, ctx)
        ye = sb("ye", [P, 2, S, TOPK, H], F32, ctx)
        xf = sb("xf", [P, 2, S, H], F32, ctx)
        f = sb("f", [P, S, H], F32, ctx)
        fg = sb("fg", [P, S, H], F32, ctx)
        yo = sb("yo", [P, 2, S, H], F32, ctx)
        ffn = Ffn("s_", sb, psum, sem, ctx)
        psD = [psum(f"s_psD{s}", ctx) for s in range(S)]

        row4_ready = sem("s_row4_ready", ctx)
        shifted = sem("s_shifted", ctx)
        ex_ready = sem("s_ex_ready", ctx)
        w4_ready = sem("s_w4_ready", ctx)
        x_in = [sem(f"s_x_in{i}", ctx) for i in range(2)]
        y_out = [sem(f"s_y_out{i}", ctx) for i in range(2)]
        ye_in = [sem(f"s_ye_in{i}", ctx) for i in range(2)]
        rows_set = sem("s_rows_set", ctx)
        taken = sem("s_taken", ctx)
        f_ready = sem("s_f_ready", ctx)
        fg_ready = sem("s_fg_ready", ctx)
        yo_ready = sem("s_yo_ready", ctx)
        own = sem("s_dve_own", ctx)
        passed = {k: sem(f"s_passed_{k}", ctx) for k in ("dve", "act", "pool")}
        GATHER = 16 * S * TOPK

        with nc.Block() as block:

            @block.sync
            def _(sp):
                for p in range(2):
                    sp.sem_inc(y_out[p], 16)
                    sp.dma_start(xf[:, p], x_v[p]).then_inc(x_in[p], 16)
                with sp.Fori(0, NU // 2) as n2:
                    for p in range(2):
                        n = n2 * 2 + p
                        sp.wait_ge(yo_ready, n + 3)
                        sp.dma_start(out_v[bass.ds(n, 1)].rearrange("o p s h -> p (o s) h"), yo[:, p]).then_inc(y_out[p], 16)
                        sp.dma_start(xf[:, p], x_v[bass.ds(n + 2, 1)].rearrange("o p s h -> p (o s) h")).then_inc(x_in[p], 16)
                for p in range(2):
                    sp.wait_ge(y_out[p], 16 * (NU // 2) + 16)
                    sp.wait_ge(x_in[p], 16 * (NU // 2 + 1))

            @block.gpsimd
            def _(pool):
                pool.wait_ge(row4_ready, 1)
                with pool.Fori(0, NU // 2) as n2:
                    for p in range(2):
                        n = n2 * 2 + p
                        pool.wait_ge(f_ready, n + 1)
                        pool.sem_inc(passed["pool"], 1)
                        nc.gpsimd.tensor_copy(row_u[:, p].rearrange("p (s k) -> p s k", s=S),
                                              row4[:, bass.ds(n * S, S), :]).then_inc(rows_set, 1)
                        pool.wait_ge(rows_set, n + 1)
                        pool.sem_inc(passed["pool"], 1)
                        for s in range(S):
                            for k in range(TOPK):
                                i = s * TOPK + k
                                nc.gpsimd.indirect_dma_start(
                                    ye[:, p, s, k, :], None, yg,
                                    bass.IndirectOffsetOnAxis(ap=row_u[:, p, i:i + 1].bitcast(mybir.dt.uint32), axis=0)
                                ).then_inc(ye_in[p], 16)

            @block.scalar
            def _(act):
                act.wait_ge(shifted, 1)
                nc.scalar.activation(ex[:, :, :], ex[:, :, :], ACT.Exp)
                nc.scalar.activation(gate[:, :], route["logit"][:, :, 0], ACT.Tanh, scale=0.5).then_inc(ex_ready, 1)
                act.preload_act_table(ACT.Silu)

                def gated(n):
                    act.wait_ge(f_ready, n + 3)
                    act.wait_ge(yo_ready, n + 2)
                    nc.scalar.activation(fg[:, :, :], f[:, :, :], ACT.Silu).then_inc(fg_ready, 1)

                def unit(n, before):
                    for j in range(SHARED):
                        q = n * SHARED + j
                        ffn.gate0(nc, act, q)
                        ffn.gate_rest(nc, act, q)
                        if before and j == SHARED - 1:
                            gated(n - 1)
                        ffn.high(nc, act, q)

                unit(0, False)
                with act.Fori(1, NU) as n:
                    unit(n, True)
                gated(NU - 1)

            @block.vector
            def _(dve):
                n_own = [0]

                def link(ins):
                    ins.then_inc(own, 1)
                    n_own[0] += 1
                    dve.wait_ge(own, n_own[0])

                ffn.start_vector(nc)
                nc.vector.sem_inc(taken, 1)
                nc.vector.sem_inc(f_ready, 2)
                nc.vector.sem_inc(yo_ready, 2)
                logits = route["logit"][:, :, 1:1 + E]
                for k in range(TOPK):
                    link(nc.vector.tensor_tensor(pick[:, :, :], route["slot"][:, :, :],
                                                 route["slot4"][:, :, k].unsqueeze(2).broadcast_to([P, NT, E]), ALU.is_equal))
                    link(nc.vector.tensor_tensor(pick[:, :, :], pick[:, :, :],
                                                 route["shift"][:, :].unsqueeze(1).broadcast_to([P, NT, E]), ALU.mult))
                    link(nc.vector.tensor_reduce(lmax[:, :], pick[:, :, :], AX.X, ALU.add))
                    last = nc.vector.tensor_tensor(row4[:, :, k], route["slot4"][:, :, k], lmax[:, :], ALU.add)
                    link(last)
                nc.vector.sem_inc(row4_ready, 1)
                link(nc.vector.tensor_reduce(lmax[:, :], logits, AX.X, ALU.max))
                nc.vector.tensor_tensor(ex[:, :, :], logits, lmax[:, :].unsqueeze(2).broadcast_to([P, NT, E]),
                                        ALU.subtract).then_inc(shifted, 1)
                dve.wait_ge(ex_ready, 1)
                link(nc.vector.tensor_reduce(den[:, :], ex[:, :, :], AX.X, ALU.add))
                link(nc.vector.reciprocal(den[:, :], den[:, :]))
                link(nc.vector.tensor_tensor(ex[:, :, :], ex[:, :, :], den[:, :].unsqueeze(2).broadcast_to([P, NT, E]), ALU.mult))
                for k in range(TOPK):
                    link(nc.vector.tensor_tensor(pick[:, :, :], route["slot"][:, :, :],
                                                 route["slot4"][:, :, k].unsqueeze(2).broadcast_to([P, NT, E]), ALU.is_equal))
                    link(nc.vector.tensor_tensor(pick[:, :, :], pick[:, :, :], ex[:, :, :], ALU.mult))
                    link(nc.vector.tensor_reduce(weight[:, k, :], pick[:, :, :], AX.X, ALU.add))
                link(nc.vector.tensor_scalar(gate[:, :], gate[:, :], 0.5, 0.5, ALU.mult, ALU.add))

                OWN0 = n_own[0]
                PER_UNIT = S * (TOPK + 1)

                def scalar_of(ap, t):
                    return ap[:, bass.ds(t, 1)]

                def step(n, j):
                    ffn.hidden(nc, dve, n * SHARED + j)
                    ffn.low(nc, dve, n * SHARED + j)

                def own_wait(m, k):
                    dve.wait_ge(own, m * PER_UNIT + (OWN0 + k))

                def take(m):
                    dve.wait_ge(ffn.down_ps, m * SHARED + SHARED + 1)
                    dve.wait_ge(fg_ready, m) if not isinstance(m, int) or m > 0 else None
                    for s in range(S):
                        nc.vector.tensor_scalar(f[:, s, :], psD[s][:, 0:H], scalar_of(gate, m * S + s), None,
                                                ALU.mult).then_inc(own, 1)
                    own_wait(m, 2)
                    dve.sem_inc(taken, 1)

                def add_experts(m, p, s, m_in):
                    dve.wait_ge(ye_in[p], m_in)
                    for k in range(TOPK):
                        last = nc.vector.scalar_tensor_tensor(out=f[:, s, :], in0=ye[:, p, s, k, :],
                                                              scalar=scalar_of(weight[:, k, :], m * S + s),
                                                              in1=f[:, s, :], op0=ALU.mult, op1=ALU.add)
                        last.then_inc(own, 1)
                        own_wait(m, 2 + s * TOPK + k + 1)
                    if s == S - 1:
                        dve.sem_inc(f_ready, 1)

                def finish(m, p, m_in):
                    dve.wait_ge(fg_ready, m + 1)
                    nc.vector.tensor_tensor(fg[:, :, :], fg[:, :, :], s_sb[:, bass.ds(m * S, S), :], ALU.mult).then_inc(passed["dve"], 1)
                    dve.wait_ge(passed["dve"], m + 1)
                    dve.wait_ge(x_in[p], m_in)
                    dve.wait_ge(y_out[p], m_in)
                    nc.vector.tensor_tensor(yo[:, p], fg[:, :, :], xf[:, p], ALU.add).then_inc(yo_ready, 1)

                for j in range(SHARED):
                    step(0, j)

                def unit(n, m2, p):
                    m = n - 1
                    step(n, 0)
                    take(m)
                    step(n, 1)
                    add_experts(m, p, 0, m2 * GATHER + GATHER)
                    step(n, 2)
                    add_experts(m, p, 1, m2 * GATHER + GATHER)
                    step(n, 3)
                    finish(m, p, m2 * 16 + 16)

                unit(1, 0, 0)
                with dve.Fori(0, NU // 2 - 1) as m2:
                    unit(m2 * 2 + 2, m2, 1)
                    unit(m2 * 2 + 3, m2 + 1, 0)
                m = NU - 1
                take(m)
                for s in range(S):
                    add_experts(m, 1, s, (m // 2) * GATHER + GATHER)
                finish(m, 1, (m // 2) * 16 + 16)

            @block.tensor
            def _(pe):
                ffn.start_tensor(pe)

                def up(n, j):
                    cols = bass.ds(n * T, T)
                    ffn.up(nc, pe, n * SHARED + j, wsh_hi[:, j], wsh_lo[:, j], lambda k: xT_hi[:, k, cols], lambda k: xT_lo[:, k, cols])

                def down(n, j):
                    if j == 0:
                        pe.wait_ge(taken, n + 1)
                    ffn.down(nc, pe, n * SHARED + j, wsh_hi[:, j], wsh_lo[:, j], [psD[s][:, 0:H] for s in range(S)],
                             first=j == 0, last_of_sum=j == SHARED - 1)

                up(0, 0)
                with pe.Fori(0, NU - 1) as n:
                    for j in range(1, SHARED):
                        up(n, j)
                        down(n, j - 1)
                    up(n + 1, 0)
                    down(n, SHARED - 1)
                for j in range(1, SHARED):
                    up(NU - 1, j)
                    down(NU - 1, j - 1)
                down(NU - 1, SHARED - 1)


def kernel(**inputs):
    import numpy as np
    import concourse.bacc as bacc
    from concourse.bass_utils import run_bass_kernel_spmd

    a = {k: np.asarray(v) for k, v in inputs.items()}
    x = a["L0_attn_x"]
    B, L, _ = x.shape
    f = x.dtype

    def zeros(*shape):
        return np.zeros(shape, f)

    def by_chunk(w):
        return np.ascontiguousarray(w.reshape(KC, P, -1).transpose(1, 0, 2).reshape(P, -1))

    wproj = by_chunk(np.concatenate([a["L0_attn_Wk"], a["L0_attn_Wv"], a["L0_attn_Wu"], a["L0_ffn_sgate_w"].T,
                                     a["L0_ffn_gate_w"].T, zeros(H, 1), a["L0_attn_Wq"]], 1))
    wo = by_chunk(a["L0_attn_Wo"])
    sgu = a["L0_ffn_shared_gate_up_w"].reshape(2, SHARED, I, H).transpose(1, 0, 2, 3)
    gu = np.concatenate([a["L0_ffn_w13"].reshape(E, 2, I, H), sgu], 0)
    dn = np.concatenate([a["L0_ffn_w2"], a["L0_ffn_shared_down_w"].reshape(H, SHARED, I).transpose(1, 0, 2)], 0)
    guT = gu.transpose(0, 3, 1, 2)
    pad = zeros(NE, H, P // 2 - IR)
    up = np.concatenate([guT[:, :, 0, :P], guT[:, :, 0, P:], pad, guT[:, :, 1, P:], pad, guT[:, :, 1, :P]], 2)
    up = up.reshape(NE, KC, P, NUP).transpose(0, 2, 1, 3).reshape(NE, P, CD)
    dT = dn.transpose(0, 2, 1)
    rest = np.concatenate([dT[:, P:], zeros(NE, P // 2 - IR, H)], 1)
    wffn = np.ascontiguousarray(np.concatenate([up, dT[:, :P], np.concatenate([rest, rest], 1)], 2))
    head = np.arange(P) // HEAD
    NTOK = B * L
    consts = np.concatenate([
        np.eye(P), (head[:, None] == head[None, :]) / float(HEAD), np.triu(np.ones((P, P)), 1),
        np.tile(1.0 + np.arange(E) * (NTOK + T), (P, 1)),
        np.tile(np.arange(NTILE) * float(T), (P, 1))], 1).astype(np.float32)
    xp = np.concatenate([x.reshape(B * L, H), zeros(2 * T, H)], 0)

    nc = bacc.Bacc("TRN2", target_bir_lowering=False, num_devices=1)
    arrays = {"x": xp, "wproj": wproj, "wo": wo, "wffn": wffn, "consts": consts}
    args = [nc.dram_tensor(n, v.shape, mybir.dt.from_np(v.dtype), kind="ExternalInput").ap() for n, v in arrays.items()]
    out = nc.dram_tensor("out", (B * L, H), F32, kind="ExternalOutput").ap()
    build(nc, *args, out)
    r = run_bass_kernel_spmd(nc, [arrays], core_ids=[0])
    return r.results[0]["out"].reshape(B, L, H)
```

```python
from contextlib import ExitStack

import concourse.bass as bass
from concourse import mybir

ALU = mybir.AluOpType
ACT = mybir.ActivationFunctionType
AX = mybir.AxisListType
F32 = mybir.dt.float32
R32 = mybir.dt.float32r
BF16 = mybir.dt.bfloat16
I32 = mybir.dt.int32

P = 128
HALF = P // 2
H = 256
KC = H // P
T = 256
S = T // P
HEAD = 16
E = 16
I = 176
SHARED = 4
NE = E + SHARED
IR = I - P
EPS = 1e-5
TOPK = 4
NONE = -3.0e38
MAGIC = float(0x5F3759DF)

CK, CV, CU, CG, CQ = 0, 256, 512, 768, 786
NG = CQ - CG
NPROJ = CQ + 256
NUP = 3 * P
CD = KC * NUP
NW = CD + 2 * H
NTOKENS = 4096
MAXTILE = NTOKENS * TOPK // T + E
MINTILE = NTOKENS * TOPK // T
NTILE = MAXTILE + 4
KI, KM, KL, KE, KR = 0, P, 2 * P, 3 * P, 3 * P + E
NCONST = KR + NTILE


def build(nc, x, wproj, wo, wffn, consts, out):
    NT = out.shape[0] // P
    NU = NT // S
    NB = 4
    UB = NU // NB
    TB = UB * S
    CAP = NU * T + T

    with ExitStack() as top:
        def psum(name, ctx, banks=1):
            return ctx.enter_context(nc.psum_tensor(name, [P, banks * 512], F32))

        def sem(name, ctx):
            return ctx.enter_context(nc.semaphore(name))

        def sb(name, shape, dt, ctx):
            return ctx.enter_context(nc.sbuf_tensor(name, shape, dt))

        xg = nc.dram_tensor("xg", (E * CAP, H), F32, kind="Internal").ap()
        yg = nc.dram_tensor("yg", (MAXTILE * T, H), F32, kind="Internal").ap()
        xnd = nc.dram_tensor("xnd", (NU * T, H), F32, kind="Internal").ap()

        xT_hi = sb("xT_hi", [P, KC, NU * T], R32, top)
        xT_lo = sb("xT_lo", [P, KC, NU * T], R32, top)
        s_sb = sb("s_sb", [P, NT, H], F32, top)
        ident = sb("ident", [P, P], F32, top)
        w_raw = sb("w_raw", [P, 2, NW], F32, top)
        w_hi = sb("w_hi", [P, 2, NW], R32, top)
        w_lo = sb("w_lo", [P, 2, NW], R32, top)
        route = {
            "slot": sb("slot", [P, NT, E], F32, top),
            "shift": sb("shift", [P, E], F32, top),
            "count": sb("count", [P, E], F32, top),
            "count_i": sb("count_i", [P, E], I32, top),
            "first": sb("first", [P, E + 1], I32, top),
            "tile_row": sb("tile_row", [P, NTILE], I32, top),
            "row4": sb("row4", [P, NT, TOPK], I32, top),
            "weight": sb("weight", [P, TOPK, NT], F32, top),
            "gate": sb("gate", [P, NT], F32, top),
        }

        x_v = x.rearrange("(n s p) h -> n p s h", s=S, p=P)
        out_v = out.rearrange("(n s p) h -> n p s h", s=S, p=P)

        attention(nc, sb, psum, sem, x_v, wproj, wo, wffn, w_raw, w_hi, w_lo, consts, xnd, xg, yg, xT_hi, xT_lo, s_sb, route, ident, NT, NB, UB, TB, CAP)
        with ExitStack() as mid:
            wsh_hi = sb("wsh_hi", [P, SHARED, NW], R32, mid)
            wsh_lo = sb("wsh_lo", [P, SHARED, NW], R32, mid)
            routed_experts(nc, sb, psum, sem, wffn, w_raw, w_hi, w_lo, xg, yg, route, wsh_hi, wsh_lo, ident, NT, CAP)
            shared_and_finish(nc, sb, psum, sem, w_raw, wsh_hi, wsh_lo, x_v, yg, xT_hi, xT_lo, s_sb, route, out_v, NT, NU)


def rsqrt_steps(nc, link, v, vh, i32, y, t, between=lambda i: None):
    def then(ins, i):
        link(ins, lambda: between(i))

    nc.vector.tensor_scalar(vh, v, -0.5, None, ALU.mult)
    then(nc.vector.tensor_scalar(i32, v.bitcast(I32), 1, None, ALU.logical_shift_right), 0)
    then(nc.vector.tensor_scalar(y.bitcast(I32), i32, -1.0, MAGIC, ALU.mult, ALU.add), 1)
    for i in range(3):
        then(nc.vector.tensor_tensor(t, vh, y, ALU.mult), 3 * i + 2)
        then(nc.vector.tensor_tensor(t, t, y, ALU.mult), 3 * i + 3)
        then(nc.vector.scalar_tensor_tensor(out=y, in0=t, scalar=1.5, in1=y, op0=ALU.add, op1=ALU.mult), 3 * i + 4)


RSQRT_LINKS = 11


def attention(nc, sb, psum, sem, x_v, wproj, wo, wffn, w_raw, w_hi, w_lo, consts, xnd, xg, yg, xT_hi, xT_lo, s_sb, route, ident, NT, NB, UB, TB, CAP):
    DEAL = 16 * TOPK * TB
    with ExitStack() as ctx:
        mask = sb("mask", [P, P], F32, ctx)
        wp_raw, wp_hi, wp_lo = (w[:, :, :].rearrange("p e n -> p (e n)")[:, 0:KC * NPROJ] for w in (w_raw, w_hi, w_lo))
        wp_hi, wp_lo = (w.rearrange("p (k n) -> p k n", k=KC) for w in (wp_hi, wp_lo))
        wo_sb = sb("wo_sb", [P, KC * H], F32, ctx)
        xin = sb("xin", [P, 2, S, H], F32, ctx)
        xn = sb("xn", [P, 2, S, H], F32, ctx)
        xs_hi = sb("xs_hi", [P, 2, KC, T], R32, ctx)
        xs_lo = sb("xs_lo", [P, 2, KC, T], R32, ctx)
        stats = sb("stats", [P, S, 6], F32, ctx)
        mv = sb("mv", [P, S, 2], F32, ctx)
        var = sb("var", [P, S], F32, ctx)
        varh = sb("varh", [P, S], F32, ctx)
        vari = sb("vari", [P, S], I32, ctx)
        rstd = sb("rstd", [P, S], F32, ctx)
        vart = sb("vart", [P, S], F32, ctx)
        k_sb = sb("k_sb", [P, S, H], F32, ctx)
        v_sb = sb("v_sb", [P, S, H], F32, ctx)
        q_sb = sb("q_sb", [P, KC, UB * T], F32, ctx)
        kvm = sb("kvm", [P, KC, P], F32, ctx)
        u_sb = sb("u_sb", [P, TB, H], F32, ctx)
        sq = sb("sq", [P, 2, H], F32, ctx)
        ms = sb("ms", [P, TB * HEAD], F32, ctx)
        msh = sb("msh", [P, TB * HEAD], F32, ctx)
        msi = sb("msi", [P, TB * HEAD], I32, ctx)
        mst = sb("mst", [P, TB * HEAD], F32, ctx)
        rn = sb("rn", [P, TB * HEAD], F32, ctx)
        at = sb("at", [P, TB, H], F32, ctx)
        aT = sb("aT", [P, 2, KC, P], F32, ctx)
        lg = sb("lg", [P, TB, 25], F32, ctx)
        top8 = sb("top8", [P, TB, 8], F32, ctx)
        rp = sb("rp", [P, TB, 24], F32, ctx)
        tri = sb("tri", [P, P], BF16, ctx)
        tri_f = sb("tri_f", [P, P], F32, ctx)
        ones = sb("ones", [P, P], BF16, ctx)
        ebase = sb("ebase", [P, E], F32, ctx)
        chosen = sb("chosen", [P, TB, E], BF16, ctx)
        before = sb("before", [P, E], F32, ctx)
        slots = sb("slots", [P, TB, E], F32, ctx)
        slot8 = sb("slot8", [P, TB, 8], F32, ctx)
        row_b = sb("row_b", [P, TB, TOPK], I32, ctx)
        prob = sb("prob", [P, TB, E], F32, ctx)
        pick4 = sb("pick4", [P, TB, TOPK, E], F32, ctx)
        den = sb("den", [P, TB], F32, ctx)
        w0_raw = q_sb[:, :, :].rearrange("p k n -> p (k n)")[:, 0:NW]
        zero = sb("zero", [P, S, H], F32, ctx)
        start = sb("start", [P, NTILE], F32, ctx)
        tmp = {"tile_i": sb("tile_i", [P, E], I32, ctx), "tiles": sb("tiles", [P, E], F32, ctx),
               "firstf": sb("firstf", [P, E + 1], F32, ctx), "step": sb("step", [P, E], F32, ctx),
               "cmp": u_sb[:, :, :].rearrange("p t h -> p (t h)")[:, 0:NTILE * E].rearrange("p (g e) -> p g e", e=E),
               "row": sb("row", [P, NTILE], F32, ctx), "cap": CAP}
        xrow = wp_raw[:, 0:TB * H].rearrange("p (t h) -> p t h", t=TB)

        psX = psum("psX", ctx)
        psKV = [psum(f"psKV{i}", ctx) for i in range(2)]
        psUG = [psum(f"psUG{i}", ctx) for i in range(2)]
        psQ = psum("psQ", ctx)
        psA = [psum(f"psA{i}", ctx) for i in range(2)]
        psT = [psX, psQ]

        s_w = sem("a_w", ctx)
        w_hi_done = sem("a_w_hi", ctx)
        w_done = sem("a_w_done", ctx)
        x_in = [sem(f"a_x_in{i}", ctx) for i in range(2)]
        x_copied = [sem(f"a_x_copied{i}", ctx) for i in range(2)]
        xn_ready = sem("a_xn_ready", ctx)
        xT_ps = sem("a_xT_ps", ctx)
        xh_ready = sem("a_xh_ready", ctx)
        xs_ready = sem("a_xs_ready", ctx)
        kv_ps = sem("a_kv_ps", ctx)
        kv_ready = sem("a_kv_ready", ctx)
        ug_ps = sem("a_ug_ps", ctx)
        u_ready = sem("a_u_ready", ctx)
        q_ps = sem("a_q_ps", ctx)
        q_ready = sem("a_q_ready", ctx)
        unit_out = sem("a_unit_out", ctx)
        kva_ps = sem("a_kva_ps", ctx)
        kvb_ready = sem("a_kvb_ready", ctx)
        o_ps = sem("a_o_ps", ctx)
        sq_ready = sem("a_sq_ready", ctx)
        p_done = sem("a_p_done", ctx)
        at_ready = sem("a_at_ready", ctx)
        aT_ps = sem("a_aT_ps", ctx)
        aT_ready = sem("a_aT_ready", ctx)
        s_ps = sem("a_s_ps", ctx)
        s_done = sem("a_s_done", ctx)
        xn_stored = [sem(f"a_xn_stored{i}", ctx) for i in range(2)]
        row_in = sem("a_row_in", ctx)
        dealt = sem("a_dealt", ctx)
        chosen_ready = sem("a_chosen", ctx)
        rank_ps = sem("a_rank_ps", ctx)
        rank_read = sem("a_rank_read", ctx)
        rows_ready = sem("a_rows_ready", ctx)
        rows_free = sem("a_rows_free", ctx)
        consts_set = sem("a_consts_set", ctx)
        counts_ready = sem("a_counts_ready", ctx)
        tails = sem("a_tails", ctx)
        cleared = sem("a_cleared", ctx)
        ident_in = sem("a_ident_in", ctx)
        wp_in = sem("a_wp_in", ctx)
        w0_in = sem("a_w0_in", ctx)
        w0_high = sem("a_w0_high", ctx)
        w0_ready = sem("a_w0_ready", ctx)
        shifted = sem("a_shifted", ctx)
        ex_ready = sem("a_ex_ready", ctx)
        dve_own = sem("a_dve_own", ctx)
        dve_passed = sem("a_dve_passed", ctx)
        pool_passed = sem("a_pool_passed", ctx)
        sp_passed = sem("a_sp_passed", ctx)

        with nc.Block() as block:

            @block.sync
            def _(sp):
                for p in range(2):
                    sp.sem_inc(x_copied[p], 16)
                sp.dma_start(ident[:, :], consts[:, KI:KI + P]).then_inc(ident_in, 16)
                sp.dma_start(xin[:, 0], x_v[0]).then_inc(x_in[0], 16)
                sp.dma_start(wp_raw, wproj).then_inc(wp_in, 16)
                sp.dma_start(xin[:, 1], x_v[1]).then_inc(x_in[1], 16)
                sp.dma_start(mask[:, :], consts[:, KM:KM + P]).then_inc(s_w, 16)
                sp.dma_start(wo_sb[:, :], wo).then_inc(s_w, 16)
                sp.dma_start(tri_f[:, :], consts[:, KL:KL + P]).then_inc(s_w, 16)
                sp.dma_start(ebase[:, :], consts[:, KE:KE + E]).then_inc(s_w, 16)
                sp.dma_start(start[:, :], consts[:, KR:KR + NTILE]).then_inc(s_w, 16)
                sp.sem_inc(rows_free, 1)
                for p in range(2):
                    sp.sem_inc(xn_stored[p], 16)
                sp.wait_ge(consts_set, 1)
                sp.wait_ge(w_done, 1)
                with sp.Fori(0, NB) as b:
                    for u in range(UB):
                        n, p = b * UB + u, u % 2
                        sp.wait_ge(xn_ready, n + 1)
                        sp.dma_start(xnd[bass.ds(n * T, T), :].rearrange("(s p) h -> p s h", p=P), xn[:, p]).then_inc(xn_stored[p], 16)
                        sp.dma_start(xin[:, p], x_v[bass.ds(n + 2, 1)].rearrange("o p s h -> p (o s) h")).then_inc(x_in[p], 16)
                        sp.wait_ge(xs_ready, n + 1)
                        sp.dma_start(f32(xT_hi[:, :, bass.ds(n * T, T)]), f32(xs_hi[:, p])).then_inc(x_copied[p], 16)
                        sp.dma_start(f32(xT_lo[:, :, bass.ds(n * T, T)]), f32(xs_lo[:, p])).then_inc(x_copied[p], 16)
                    for p in range(2):
                        sp.wait_ge(xn_stored[p], b * (16 * UB // 2) + 16 * UB // 2 + 16)
                        sp.sem_inc(sp_passed, 1)
                    for i in range((MAXTILE - MINTILE) // NB):
                        sp.dma_start(yg[bass.ds(b * ((MAXTILE - MINTILE) // NB * T) + (MINTILE + i) * T, T), :]
                                     .rearrange("(s p) h -> p s h", p=P), zero[:, :, :]).then_inc(cleared, 16)
                    sp.wait_ge(rows_free, b + 1)
                    sp.sem_inc(sp_passed, 1)
                    sp.dma_start(xrow, xnd[bass.ds(b * (TB * P), TB * P), :].rearrange("(t p) h -> p t h", p=P)).then_inc(row_in, 16)
                sp.wait_ge(o_ps, NB * TB)
                sp.dma_start(w0_raw, wffn[0]).then_inc(w0_in, 16)
                sp.wait_ge(counts_ready, NB)
                with sp.Fori(0, E) as e:
                    n_e = sp.value_load(route["count_i"][0:1, bass.ds(e, 1)], min_val=0, max_val=NTOKENS)
                    sp.dma_start(xg[bass.ds(e * CAP + n_e, T), :].rearrange("(s p) h -> p s h", p=P), zero[:, :, :]).then_inc(tails, 16)
                sp.wait_ge(tails, 16 * E)
                sp.wait_ge(cleared, 16 * (MAXTILE - MINTILE))
                for p in range(2):
                    sp.wait_ge(x_copied[p], 32 * (NB * UB // 2) + 16)
                    sp.wait_ge(x_in[p], 16 * (NB * UB // 2 + 1))

            @block.gpsimd
            def _(pool):
                nc.gpsimd.memset(zero[:, :, :], 0.0)
                nc.gpsimd.memset(ones[:, :], 1.0).then_inc(consts_set, 1)
                with pool.Fori(0, NB) as b:
                    pool.wait_ge(rows_ready, b + 1)
                    pool.wait_ge(row_in, b * 16 + 16)
                    pool.sem_inc(pool_passed, 1)
                    for t in range(TB):
                        for k in range(TOPK):
                            nc.gpsimd.indirect_dma_start(
                                xg, bass.IndirectOffsetOnAxis(ap=row_b[:, t, k:k + 1].bitcast(mybir.dt.uint32), axis=0),
                                xrow[:, t, :], None).then_inc(dealt, 16)
                    pool.wait_ge(dealt, b * DEAL + DEAL)
                    pool.sem_inc(rows_free, 1)

            @block.scalar
            def _(act):
                nc.scalar.sem_inc(s_done, 1)
                act.preload_act_table(ACT.Silu)
                act.wait_ge(wp_in, 16)
                nc.scalar.copy(wp_hi[:, :, :].rearrange("p k n -> p (k n)"), wp_raw).then_inc(w_hi_done, 1)
                act.wait_ge(xT_ps, 1)
                nc.scalar.copy(xs_hi[:, 0].rearrange("p k t -> p (k t)"), psX[:, :]).then_inc(xh_ready, 1)
                with act.Fori(0, NB) as b:
                    for u in range(UB):
                        n, p = b * UB + u, u % 2
                        for s in range(S):
                            act.wait_ge(kv_ps, n * S + s + 1)
                            nc.scalar.activation(k_sb[:, s], psKV[s][:, 0:H], ACT.Relu)
                            nc.scalar.copy(v_sb[:, s], psKV[s][:, H:2 * H]).then_inc(kv_ready, 1)
                        for s in range(S):
                            act.wait_ge(ug_ps, n * S + s + 1)
                            nc.scalar.activation(u_sb[:, u * S + s, :], psUG[s][:, 0:H], ACT.Silu).then_inc(u_ready, 1)
                        act.wait_ge(xT_ps, n + 2)
                        act.wait_ge(x_copied[1 - p], b * (32 * UB // 2) + 32 * ((u + 1) // 2) + 16)
                        nc.scalar.copy(xs_hi[:, 1 - p].rearrange("p k t -> p (k t)"), psX[:, :]).then_inc(xh_ready, 1)
                        act.wait_ge(q_ps, n + 1)
                        nc.scalar.activation(q_sb[:, :, u * T:(u + 1) * T],
                                             psQ[:, :].rearrange("p (k t) -> p k t", k=KC), ACT.Relu).then_inc(q_ready, 1)
                    for t in range(TB):
                        act.wait_ge(o_ps, b * TB + t + 1)
                        nc.scalar.activation(sq[:, t % 2], psKV[t % 2][:, 0:H], ACT.Square).then_inc(sq_ready, 1)

                    def head_out(t):
                        act.wait_ge(s_ps, b * TB + t + 1)
                        nc.scalar.copy(s_sb[:, bass.ds(b * TB + t, 1), :].rearrange("p o h -> p (o h)"),
                                       psUG[t % 2][:, 0:H]).then_inc(s_done, 1)

                    for t in range(TB):
                        act.wait_ge(aT_ps, b * TB + t + 1)
                        nc.scalar.copy(aT[:, t % 2].rearrange("p k t -> p (k t)"), psT[t % 2][:, 0:H]).then_inc(aT_ready, 1)
                        if t:
                            head_out(t - 1)
                    head_out(TB - 1)
                    act.wait_ge(shifted, b + 1)
                    nc.scalar.activation(prob[:, :, :], prob[:, :, :], ACT.Exp)
                    nc.scalar.activation(route["gate"][:, bass.ds(b * TB, TB)], lg[:, :, 0], ACT.Tanh, scale=0.5).then_inc(ex_ready, 1)
                act.wait_ge(w0_in, 16)
                nc.scalar.copy(w_hi[:, 0], w0_raw).then_inc(w0_high, 1)

            @block.vector
            def _(dve):
                count = [0, 0]

                def link(ins, meanwhile=None):
                    ins.then_inc(dve_own, 1)
                    count[1] += 1
                    made = count[0] + count[1]
                    if meanwhile:
                        meanwhile()
                    dve.wait_ge(dve_own, made)

                def normalise(m_in, p, stored=None):
                    dve.wait_ge(x_in[p], m_in)
                    for s in range(S):
                        last = nc.vector.bn_stats(stats[:, s, :], xin[:, p, s, :])
                    link(last)
                    dve.sem_inc(dve_passed, 1)
                    for s in range(S):
                        last = nc.vector.bn_aggr(mv[:, s, :], stats[:, s, :])
                    link(last)
                    link(nc.vector.tensor_scalar(var[:, :], mv[:, :, 1], EPS, None, ALU.add))
                    rsqrt_steps(nc, link, var[:, :], varh[:, :], vari[:, :], rstd[:, :], vart[:, :])
                    if stored is not None:
                        dve.wait_ge(xn_stored[p], stored)
                    for s in range(S):
                        last = nc.vector.tensor_scalar(xn[:, p, s, :], xin[:, p, s, :], mv[:, s, 0:1],
                                                       rstd[:, s:s + 1], ALU.subtract, ALU.mult)
                    last.then_inc(xn_ready, 1)

                def split_x(p):
                    nc.vector.tensor_tensor(xs_lo[:, p].rearrange("p k t -> p (k t)"), psX[:, :],
                                            f32(xs_hi[:, p].rearrange("p k t -> p (k t)")), ALU.subtract).then_inc(xs_ready, 1)

                nc.vector.sem_inc(unit_out, 1)
                nc.vector.sem_inc(rank_read, 1)
                nc.vector.memset(lg[:, :, :], NONE)
                normalise(16, 0)
                dve.wait_ge(w_hi_done, 1)
                nc.vector.tensor_tensor(wp_lo[:, :, :].rearrange("p k n -> p (k n)"), wp_raw,
                                        f32(wp_hi[:, :, :].rearrange("p k n -> p (k n)")), ALU.subtract).then_inc(w_done, 1)
                dve.wait_ge(s_w, 80)
                nc.vector.tensor_copy(before[:, :], ebase[:, :])
                nc.vector.tensor_copy(tri[:, :], tri_f[:, :])
                dve.wait_ge(xh_ready, 1)
                split_x(0)
                normalise(16, 1)
                LINKS0 = count[1]
                links_per_seq = UB * (3 + RSQRT_LINKS) + 3 + 2 * (1 + RSQRT_LINKS) + 1 + 4
                with dve.Fori(0, NB) as b:
                    count[0], count[1] = LINKS0 + b * links_per_seq, 0

                    def normalise_next(u):
                        normalise(b * (16 * UB // 2) + 16 * (u // 2 + 2), u % 2, b * (16 * UB // 2) + 16 * (u // 2 + 1) + 16)

                    for u in range(UB):
                        n, p = b * UB + u, u % 2
                        for s in range(S):
                            dve.wait_ge(u_ready, n * S + s + 1)
                            last = nc.vector.tensor_copy(lg[:, u * S + s, 0:17], psUG[s][:, H:H + 17])
                        last.then_inc(unit_out, 1)
                        dve.wait_ge(xh_ready, n + 2)
                        split_x(1 - p)
                        if u < UB - 1:
                            normalise_next(u)
                    dve.wait_ge(unit_out, b * UB + (UB + 1))
                    dve.sem_inc(dve_passed, 1)
                    for t in range(TB):
                        last = nc.vector.max(top8[:, t, :], lg[:, t, 1:17])
                    link(last)
                    def keep_heads():
                        dve.wait_ge(kva_ps, b * UB + UB)
                        for c in range(KC):
                            last = nc.vector.tensor_tensor(kvm[:, c], psA[c][:, 0:P], mask[:, :], ALU.mult)
                        last.then_inc(kvb_ready, 1)

                    link(nc.vector.memset(top8[:, :, 4:8], NONE), keep_heads)
                    dve.sem_inc(dve_passed, 1)
                    for t in range(TB):
                        last = nc.vector.match_replace(rp[:, t, :], top8[:, t, :], lg[:, t, 1:25], NONE)
                    link(last)
                    nc.vector.tensor_tensor(chosen[:, :, :], rp[:, :, 0:E], lg[:, :, 1:17], ALU.not_equal).then_inc(chosen_ready, 1)
                    nc.vector.tensor_tensor(prob[:, :, :], lg[:, :, 1:17], top8[:, :, 0:1].broadcast_to([P, TB, E]),
                                            ALU.subtract).then_inc(shifted, 1)

                    def mean_square(t):
                        dve.wait_ge(sq_ready, b * TB + t + 1)
                        nc.vector.tensor_reduce(ms[:, t * HEAD:(t + 1) * HEAD],
                                                sq[:, t % 2].rearrange("p (h d) -> p h d", d=HEAD), AX.X, ALU.add)
                        nc.vector.tensor_tensor(u_sb[:, t, :], psKV[t % 2][:, 0:H], u_sb[:, t, :], ALU.mult).then_inc(p_done, 1)

                    def normed(t):
                        nc.vector.tensor_tensor(
                            at[:, t].rearrange("p (h d) -> p h d", d=HEAD),
                            u_sb[:, t, :].rearrange("p (h d) -> p h d", d=HEAD),
                            rn[:, t * HEAD:(t + 1) * HEAD].unsqueeze(2).broadcast_to([P, HEAD, HEAD]),
                            ALU.mult).then_inc(at_ready, 1)

                    def inverse_norms(g, between):
                        cols = slice(g * TB // 2 * HEAD, (g + 1) * TB // 2 * HEAD)
                        dve.wait_ge(p_done, b * TB + (g + 1) * TB // 2)
                        dve.sem_inc(dve_passed, 1)
                        link(nc.vector.tensor_scalar(ms[:, cols], ms[:, cols], 1.0 / HEAD, 1e-24, ALU.mult, ALU.max))
                        rsqrt_steps(nc, link, ms[:, cols], msh[:, cols], msi[:, cols], rn[:, cols], mst[:, cols], between)

                    def deal():
                        dve.wait_ge(rank_ps, b + 1)
                        nc.vector.tensor_copy(before[:, :], psA[0][:, TB * E:(TB + 1) * E])
                        nc.vector.tensor_tensor(slots[:, :, :], psA[0][:, 0:TB * E].rearrange("p (t e) -> p t e", e=E),
                                                chosen[:, :, :], ALU.mult).then_inc(rank_read, 1)
                        dve.wait_ge(rank_read, b + 2)
                        dve.sem_inc(dve_passed, 1)
                        nc.vector.tensor_tensor(route["count_i"][:, :], before[:, :], ebase[:, :],
                                                ALU.subtract).then_inc(counts_ready, 1)
                        for t in range(TB):
                            last = nc.vector.max(slot8[:, t, :], slots[:, t, :])
                        link(last, lambda: nc.vector.tensor_copy(route["slot"][:, bass.ds(b * TB, TB), :], slots[:, :, :]))
                        dve.wait_ge(rows_free, b + 1)
                        dve.sem_inc(dve_passed, 1)
                        nc.vector.tensor_scalar(row_b[:, :, :], slot8[:, :, 0:TOPK], 1.0, None, ALU.subtract).then_inc(rows_ready, 1)

                    HT = TB // 2
                    for t in range(HT):
                        mean_square(t)
                    deal()
                    inverse_norms(0, lambda i: mean_square(HT + i // 3) if i % 3 == 0 else None)
                    inverse_norms(1, lambda i: normed(i // 2) if i % 2 == 0 and i // 2 < HT else None)
                    for t in range(HT, TB):
                        normed(t)
                    normalise_next(UB - 1)
                    dve.wait_ge(ex_ready, b + 1)
                    link(nc.vector.tensor_reduce(den[:, :], prob[:, :, :], AX.X, ALU.add))
                    nc.vector.tensor_tensor(pick4[:, :, :, :], slots[:, :, :].unsqueeze(2).broadcast_to([P, TB, TOPK, E]),
                                            slot8[:, :, 0:TOPK].unsqueeze(3).broadcast_to([P, TB, TOPK, E]), ALU.is_equal)
                    link(nc.vector.reciprocal(den[:, :], den[:, :]))
                    link(nc.vector.tensor_tensor(prob[:, :, :], prob[:, :, :], den[:, :].unsqueeze(2).broadcast_to([P, TB, E]),
                                                 ALU.mult))
                    link(nc.vector.tensor_tensor(pick4[:, :, :, :], pick4[:, :, :, :],
                                                 prob[:, :, :].unsqueeze(2).broadcast_to([P, TB, TOPK, E]), ALU.mult))
                    nc.vector.tensor_reduce(route["weight"][:, :, bass.ds(b * TB, TB)].rearrange("p k t -> p t k"),
                                            pick4[:, :, :, :], AX.X, ALU.add)
                    gate_b = route["gate"][:, bass.ds(b * TB, TB)]
                    nc.vector.tensor_scalar(gate_b, gate_b, 0.5, 0.5, ALU.mult, ALU.add)
                    assert count[1] == links_per_seq, count[1]
                count[0], count[1] = LINKS0 + NB * links_per_seq, 0
                dve.wait_ge(s_w, 80)
                link(nc.vector.tensor_tensor(route["count"][:, :], before[:, :], ebase[:, :], ALU.subtract))
                link(tile_tables(nc, link, start, ebase, route, tmp))
                nc.vector.memset(f32(w_lo[HALF:P, 0, CD + H:NW]), 0.0)
                dve.wait_ge(w0_high, 1)
                split_low(nc.vector, w0_raw, w_hi[:, 0], w_lo[:, 0]).then_inc(w0_ready, 1)

            @block.tensor
            def _(pe):
                def transpose_x(p):
                    for k in range(KC):
                        for s in range(S):
                            last = nc.tensor.transpose(psX[:, k * T + s * P:k * T + (s + 1) * P],
                                                       xn[:, p, s, k * P:(k + 1) * P], ident[:, :])
                    last.then_inc(xT_ps, 1)

                def products(out, lhs, rhs):
                    i = 0
                    for k in range(len(lhs)):
                        (ah, al), (bh, bl) = lhs[k], rhs[k]
                        for a, c in ((ah, bh), (ah, bl), (al, bh)):
                            last = nc.tensor.matmul(out, a, c, start=i == 0, stop=i == 3 * len(lhs) - 1)
                            i += 1
                    return last

                def wcols(k, a, n):
                    return wp_hi[:, k, a:a + n], wp_lo[:, k, a:a + n]

                pe.wait_ge(ident_in, 16)
                pe.wait_ge(xn_ready, 1)
                transpose_x(0)
                pe.wait_ge(s_w, 80)
                pe.wait_ge(w_done, 1)
                with pe.Fori(0, NB) as b:
                    for u in range(UB):
                        n, p = b * UB + u, u % 2

                        def xcols(k, a, n):
                            return xs_hi[:, p, k, a:a + n], xs_lo[:, p, k, a:a + n]

                        pe.wait_ge(xs_ready, n + 1)
                        for s in range(S):
                            products(psKV[s][:, :], [xcols(k, s * P, P) for k in range(KC)],
                                     [wcols(k, CK, 2 * H) for k in range(KC)]).then_inc(kv_ps, 1)
                        pe.wait_ge(unit_out, n + 1)
                        if u == 0:
                            pe.wait_ge(s_done, b * TB + 1)
                        for s in range(S):
                            for k in range(KC):
                                (xh, xl), (wh, wl) = xcols(k, s * P, P), wcols(k, CU, H + NG)
                                nc.tensor.matmul(psUG[s][:, 0:H + NG], xh, wh, start=k == 0, stop=False)
                                nc.tensor.matmul(psUG[s][:, 0:H + NG], xh, wl, start=False, stop=False)
                                nc.tensor.matmul(psUG[s][:, H:H + NG], xl, wl[:, H:H + NG], start=False, stop=False,
                                                 skip_group_check=True)
                                last = nc.tensor.matmul(psUG[s][:, 0:H + NG], xl, wh, start=False, stop=k == KC - 1)
                            last.then_inc(ug_ps, 1)
                        pe.wait_ge(xn_ready, n + 2)
                        transpose_x(1 - p)
                        if u > 0:
                            pe.wait_ge(q_ready, n)
                        for c in range(KC):
                            last = products(psQ[:, c * T:(c + 1) * T], [wcols(k, CQ + c * P, P) for k in range(KC)],
                                            [xcols(k, 0, T) for k in range(KC)])
                        last.then_inc(q_ps, 1)
                        pe.wait_ge(kv_ready, n * S + S)
                        if u == 0:
                            pe.wait_ge(rank_read, b + 1)
                        for s in range(S):
                            for c in range(KC):
                                kk = slice(c * P, (c + 1) * P)
                                last = nc.tensor.matmul(psA[c][:, 0:P], k_sb[:, s, kk], v_sb[:, s, kk],
                                                        start=u == 0 and s == 0, stop=u == UB - 1 and s == S - 1)
                        last.then_inc(kva_ps, 1)

                    def ranks():
                        pe.wait_ge(chosen_ready, b + 1)
                        pe.wait_ge(consts_set, 1)
                        slots_ps = psA[0][:, 0:TB * E].rearrange("p (t e) -> p t e", e=E)
                        nc.tensor.matmul(slots_ps, tri[:, :], chosen[:, :, :], start=True, stop=False)
                        for t in range(TB - 1):
                            nc.tensor.matmul(slots_ps[:, t + 1:TB, :], ones[:, :],
                                             chosen[:, t:t + 1, :].broadcast_to([P, TB - 1 - t, E]), start=False, stop=False)
                        nc.tensor.matmul(slots_ps, ident[:, :], before[:, :].unsqueeze(1).broadcast_to([P, TB, E]),
                                         start=False, stop=True)
                        for t in range(TB):
                            nc.tensor.matmul(psA[0][:, TB * E:(TB + 1) * E], ones[:, :], chosen[:, t, :], start=t == 0, stop=False)
                        nc.tensor.matmul(psA[0][:, TB * E:(TB + 1) * E], ident[:, :], before[:, :], start=False,
                                         stop=True).then_inc(rank_ps, 1)

                    pe.wait_ge(kvb_ready, b + 1)
                    pe.wait_ge(q_ready, b * UB + UB)
                    for t in range(TB):
                        if t >= 2:
                            pe.wait_ge(p_done, b * TB + t - 1)
                        for c in range(KC):
                            last = nc.tensor.matmul(psKV[t % 2][:, c * P:(c + 1) * P], q_sb[:, c, t * P:(t + 1) * P],
                                                    kvm[:, c], start=True, stop=True)
                        last.then_inc(o_ps, 1)
                        if t == 1:
                            ranks()

                    def head_out(t):
                        pe.wait_ge(aT_ready, b * TB + t + 1)
                        if t >= 2:
                            pe.wait_ge(s_done, b * TB + t)
                        for k in range(KC):
                            last = nc.tensor.matmul(psUG[t % 2][:, 0:H], aT[:, t % 2, k], wo_sb[:, k * H:(k + 1) * H],
                                                    start=k == 0, stop=k == KC - 1)
                        last.then_inc(s_ps, 1)

                    for t in range(TB):
                        pe.wait_ge(at_ready, b * TB + t + 1)
                        for k in range(KC):
                            last = nc.tensor.transpose(psT[t % 2][:, k * P:(k + 1) * P], at[:, t, k * P:(k + 1) * P],
                                                       ident[:, :])
                        last.then_inc(aT_ps, 1)
                        if t:
                            head_out(t - 1)
                    head_out(TB - 1)


def f32(ap):
    return ap.bitcast(F32)


class Ffn:

    def __init__(self, tag, sb, psum, sem, ctx, split):
        self.split = split
        self.sg0 = sb(tag + "sg0", [P, T], F32, ctx)
        self.sgm = sb(tag + "sgm", [P, T], F32, ctx)
        self.h0 = sb(tag + "h0", [P, T], F32, ctx)
        self.hm = sb(tag + "hm", [P, T], F32, ctx)
        self.h0_hi = sb(tag + "h0_hi", [P, split * T], R32, ctx)
        self.h0_lo = sb(tag + "h0_lo", [P, split * T], R32, ctx)
        self.hm_s = sb(tag + "hm_s", [P, split * T], R32, ctx)
        self.psM = psum(tag + "psM", ctx, 2)
        self.psG = psum(tag + "psG", ctx, 2)
        self.psU = psum(tag + "psU", ctx, 2)
        self.up_ps = sem(tag + "up_ps", ctx)
        self.sg_ready = sem(tag + "sg_ready", ctx)
        self.hm_made = sem(tag + "hm_made", ctx)
        self.h0_made = sem(tag + "h0_made", ctx)
        self.hh_ready = sem(tag + "hh_ready", ctx)
        self.hl_ready = sem(tag + "hl_ready", ctx)
        self.down_ps = sem(tag + "down_ps", ctx)

    @staticmethod
    def bank(r):
        return slice(r * 512, r * 512 + T) if isinstance(r, int) else bass.ds(r * 512, T)

    @staticmethod
    def half(r):
        return slice(r * T, (r + 1) * T) if isinstance(r, int) else bass.ds(r * T, T)

    def start_vector(self, nc):
        nc.vector.sem_inc(self.hm_made, 2)
        nc.vector.sem_inc(self.h0_made, 2)
        nc.vector.sem_inc(self.hl_ready, 2)

    def start_tensor(self, pe):
        pe.sem_inc(self.down_ps, self.split)

    def up(self, nc, pe, q, r, w_hi, w_lo, x_hi, x_lo, between=lambda c: None):
        for c, pair in ((1, self.psM), (0, self.psG), (2, self.psU)):
            pe.wait_ge(self.hm_made if c == 1 else self.h0_made, q + 1)
            i = 0
            for k in range(KC):
                cols = slice(k * NUP + c * P, k * NUP + (c + 1) * P)
                for w, xx in ((w_hi, x_hi), (w_hi, x_lo), (w_lo, x_hi)):
                    last = nc.tensor.matmul(pair[:, self.bank(r)], w[:, cols], xx(k), start=i == 0, stop=i == 5)
                    i += 1
            last.then_inc(self.up_ps, 1)
            between(c)

    def down(self, nc, pe, q, b, w_hi, w_lo, out, first=True, last_of_sum=True):
        pe.wait_ge(self.hl_ready, q * 2 + 4)
        d0, d1 = slice(CD, CD + H), slice(CD + H, NW)
        ops = ((self.hm_s, w_hi, d1), (self.hm_s, w_lo, d1),
               (self.h0_hi, w_hi, d0), (self.h0_hi, w_lo, d0), (self.h0_lo, w_hi, d0))
        for s in range(S):
            for i, (h, w, d) in enumerate(ops):
                at = slice(b * T + s * P, b * T + (s + 1) * P)
                last = nc.tensor.matmul(out[s], h[:, at], w[:, d], start=first and i == 0,
                                        stop=last_of_sum and i == len(ops) - 1)
        last.then_inc(self.down_ps, 1)

    def gate_rest(self, nc, act, q, r):
        act.wait_ge(self.up_ps, q * 3 + 1)
        act.wait_ge(self.hm_made, q + 2)
        nc.scalar.activation(self.sgm[0:HALF, :], self.psM[0:HALF, self.bank(r)], ACT.Silu).then_inc(self.sg_ready, 1)

    def high_rest(self, nc, act, q, b):
        act.wait_ge(self.hm_made, q + 3)
        act.wait_ge(self.down_ps, q + 1)
        nc.scalar.copy(self.hm_s[0:HALF, self.half(b)], self.hm[0:HALF, :]).then_inc(self.hh_ready, 1)

    def gate0(self, nc, act, q, r):
        act.wait_ge(self.up_ps, q * 3 + 2)
        act.wait_ge(self.h0_made, q + 2)
        nc.scalar.activation(self.sg0[:, :], self.psG[:, self.bank(r)], ACT.Silu).then_inc(self.sg_ready, 1)

    def high0(self, nc, act, q, b):
        act.wait_ge(self.h0_made, q + 3)
        nc.scalar.copy(self.h0_hi[:, self.half(b)], self.h0[:, :]).then_inc(self.hh_ready, 1)

    def hidden_rest(self, nc, dve, q, r):
        dve.wait_ge(self.sg_ready, q * 2 + 1)
        dve.wait_ge(self.hl_ready, q * 2 + 1)
        nc.vector.tensor_tensor(self.hm[0:HALF, :], self.psM[HALF:P, self.bank(r)], self.sgm[0:HALF, :],
                                ALU.mult).then_inc(self.hm_made, 1)

    def low_rest(self, nc, dve, q, b):
        dve.wait_ge(self.hh_ready, q * 2 + 1)
        nc.vector.tensor_tensor(self.hm_s[HALF:P, self.half(b)], self.hm[0:HALF, :], f32(self.hm_s[0:HALF, self.half(b)]),
                                ALU.subtract).then_inc(self.hl_ready, 1)

    def hidden0(self, nc, dve, q, r):
        dve.wait_ge(self.up_ps, q * 3 + 3)
        dve.wait_ge(self.sg_ready, q * 2 + 2)
        dve.wait_ge(self.hl_ready, q * 2 + 2)
        nc.vector.tensor_tensor(self.h0[:, :], self.psU[:, self.bank(r)], self.sg0[:, :], ALU.mult).then_inc(self.h0_made, 1)

    def low0(self, nc, dve, q, b):
        dve.wait_ge(self.hh_ready, q * 2 + 2)
        nc.vector.tensor_tensor(self.h0_lo[:, self.half(b)], self.h0[:, :], f32(self.h0_hi[:, self.half(b)]),
                                ALU.subtract).then_inc(self.hl_ready, 1)


def tile_tables(nc, link, consts_sb, ebase, route, tmp):
    tile_i, tiles, firstf, step, cmp, row = (tmp[k] for k in ("tile_i", "tiles", "firstf", "step", "cmp", "row"))
    start = consts_sb[:, :]
    link(nc.vector.tensor_scalar(tile_i[:, :], route["count"][:, :], T - 1.0, None, ALU.add))
    link(nc.vector.tensor_scalar(tile_i[:, :], tile_i[:, :], T.bit_length() - 1, None, ALU.logical_shift_right))
    link(nc.vector.tensor_scalar(tiles[:, :], tile_i[:, :], 1.0, None, ALU.max))
    sums, other = tiles, step
    for d in (1, 2, 4, 8):
        nc.vector.tensor_copy(other[:, 0:d], sums[:, 0:d])
        link(nc.vector.tensor_tensor(other[:, d:E], sums[:, d:E], sums[:, 0:E - d], ALU.add))
        sums, other = other, sums
    nc.vector.memset(firstf[:, 0:1], 0.0)
    link(nc.vector.tensor_copy(firstf[:, 1:E + 1], sums[:, :]))
    link(nc.vector.tensor_tensor(tiles[:, :], firstf[:, 1:E + 1], firstf[:, 0:E], ALU.subtract))
    link(nc.vector.tensor_copy(route["first"][:, :], firstf[:, :]))
    link(nc.vector.tensor_scalar(step[:, :], tiles[:, :], -float(T), float(tmp["cap"]), ALU.mult, ALU.add))
    link(nc.vector.tensor_scalar(firstf[:, :], firstf[:, :], float(T), None, ALU.mult))
    link(nc.vector.tensor_tensor(cmp[:, :, :], start.unsqueeze(2).broadcast_to([P, NTILE, E]),
                                 firstf[:, 1:E + 1].unsqueeze(1).broadcast_to([P, NTILE, E]), ALU.is_ge))
    link(nc.vector.tensor_tensor(cmp[:, :, :], cmp[:, :, :], step[:, :].unsqueeze(1).broadcast_to([P, NTILE, E]), ALU.mult))
    link(nc.vector.tensor_reduce(row[:, :], cmp[:, :, :], AX.X, ALU.add))
    link(nc.vector.tensor_tensor(row[:, :], row[:, :], start, ALU.add))
    link(nc.vector.tensor_scalar(cmp[:, :, 0], start, firstf[:, E:E + 1], None, ALU.is_lt))
    link(nc.vector.tensor_tensor(route["tile_row"][:, :], row[:, :], cmp[:, :, 0], ALU.mult))
    return nc.vector.tensor_tensor(route["shift"][:, :], firstf[:, 0:E], ebase[:, :], ALU.subtract)


def chosen_rows(nc, link, route, moved, there):
    NT = moved.shape[1]
    link(nc.vector.tensor_scalar(there, route["slot"][:, :, :], 0.0, None, ALU.is_gt))
    link(nc.vector.tensor_tensor(moved, route["slot"][:, :, :],
                                 route["shift"][:, :].unsqueeze(1).broadcast_to([P, NT, E]), ALU.add))
    link(nc.vector.scalar_tensor_tensor(out=moved, in0=moved, scalar=1.0, in1=there,
                                        op0=ALU.add, op1=ALU.mult))
    for t in range(NT):
        last = nc.vector.max(there[:, t, 0:8], moved[:, t, :])
    link(last)
    return nc.vector.tensor_scalar(route["row4"][:, :, :], there[:, :, 0:TOPK], 1.0, None, ALU.subtract)


def split_low(engine, raw, w_hi, w_lo):
    engine.tensor_tensor(w_lo[:, 0:CD + H], raw[:, 0:CD + H], f32(w_hi[:, 0:CD + H]), ALU.subtract)
    return engine.tensor_tensor(w_lo[0:HALF, CD + H:NW], raw[0:HALF, CD + H:NW], f32(w_hi[0:HALF, CD + H:NW]), ALU.subtract)


def split_weights(nc, pool, raw, w_hi, w_lo, own, n, done):
    nc.gpsimd.tensor_copy(w_hi, raw).then_inc(own, 1)
    pool.wait_ge(own, n)
    split_low(nc.gpsimd, raw, w_hi, w_lo).then_inc(done, 1)


def routed_experts(nc, sb, psum, sem, wffn, w_raw, w_hi, w_lo, xg, yg, route, wsh_hi, wsh_lo, ident, NT, CAP):
    with ExitStack() as ctx:
        RING = 4
        ring = sb("ring", [P, RING, S, H], F32, ctx)
        rows = sb("rows", [P, S, H], F32, ctx)
        x_hi = sb("x_hi", [P, KC, 2 * T], R32, ctx)
        x_lo = sb("x_lo", [P, KC, 2 * T], R32, ctx)
        y = sb("y", [P, 2, S * H], F32, ctx)
        moved, there = (y[:, i, :].rearrange("p (t e) -> p t e", e=E) for i in range(2))
        ffn = Ffn("e_", sb, psum, sem, ctx, 1)
        psX = psum("e_psX", ctx)
        psD = psum("e_psD", ctx)

        w_in = [sem(f"e_w_in{i}", ctx) for i in range(2)]
        zeroed = sem("e_zeroed", ctx)
        wh_done = sem("e_wh_done", ctx)
        w_split = sem("e_w_split", ctx)
        w_ready = sem("e_w_ready", ctx)
        landed = sem("e_landed", ctx)
        copied = sem("e_copied", ctx)
        xT_ps = sem("e_xT_ps", ctx)
        xh_ready = sem("e_xh_ready", ctx)
        xs_ready = sem("e_xs_ready", ctx)
        y_ready = sem("e_y_ready", ctx)
        stored = sem("e_stored", ctx)
        own = sem("e_dve_own", ctx)
        passed = {k: sem(f"e_passed_{k}", ctx) for k in ("dve", "act", "pool", "sp")}

        def over_experts(body):
            body(0, 0, True)

            def pairs(eng):
                with eng.Fori(0, E // 2 - 1) as j:
                    for p in (1, 0):
                        body(j * 2 + 2 - p, p, False)
            return pairs

        def expert_tiles(eng, e, first_tile, next_tile):
            f = route["first"]
            g0 = eng.value_load(f[0:1, bass.ds(e, 1)], min_val=0, max_val=NTILE - 5)
            g1 = eng.value_load(f[0:1, bass.ds(e + 1, 1)], min_val=1, max_val=NTILE - 4)
            first_tile(g0)
            with eng.If(g1 > g0 + 1):
                with eng.Fori(g0 + 1, g1) as g:
                    next_tile(g)

        with nc.Block() as block:

            @block.sync
            def _(sp):
                sp.sem_inc(stored, 32)
                def load(g, slot):
                    row = sp.value_load(route["tile_row"][0:1, bass.ds(g, 1)], min_val=0, max_val=E * CAP - T)
                    sp.dma_start(ring[:, slot], xg[bass.ds(row, T), :].rearrange("(s p) h -> p s h", p=P)).then_inc(landed, 16)

                for g in range(RING):
                    load(g, g)
                    sp.wait_ge(landed, 16 * (g + 1))
                tiles = sp.value_load(route["first"][0:1, E:E + 1], min_val=1, max_val=NTILE - 4)
                with sp.Fori(0, tiles) as g:
                    sp.wait_ge(copied, g + 1)
                    sp.sem_inc(passed["sp"], 1)
                    row = sp.value_load(route["tile_row"][0:1, bass.ds(g + RING, 1)], min_val=0, max_val=E * CAP - T)
                    sp.wait_ge(landed, g * 16 + 16 * RING)
                    sp.sem_inc(passed["sp"], 1)
                    sp.dma_start(ring[:, bass.ds(g % RING, 1)].rearrange("p o s h -> p (o s) h"),
                                 xg[bass.ds(row, T), :].rearrange("(s p) h -> p s h", p=P)).then_inc(landed, 16)
                    sp.wait_ge(y_ready, g + 2)
                    sp.sem_inc(passed["sp"], 1)
                    sp.wait_ge(stored, g * 16 + 32)
                    sp.sem_inc(passed["sp"], 1)
                    sp.dma_start(yg[bass.ds(g * T, T), :].rearrange("(s p) h -> p s h", p=P),
                                 y[:, bass.ds(g % 2, 1)].rearrange("p o (s h) -> p (o s) h", s=S)).then_inc(stored, 16)
                sp.wait_ge(landed, tiles * 16 + 16 * RING)
                sp.sem_inc(passed["sp"], 1)
                sp.wait_ge(stored, tiles * 16 + 32)
                sp.sem_inc(passed["sp"], 1)

            @block.gpsimd
            def _(pool):
                pool.sem_inc(w_ready, 1)
                nc.gpsimd.memset(f32(wsh_lo[HALF:P, :, CD + H:NW]), 0.0)
                nc.gpsimd.memset(f32(w_lo[HALF:P, 1, CD + H:NW]), 0.0).then_inc(zeroed, 1)
                pool.wait_ge(zeroed, 1)
                for i in (1, 2):
                    pool.dma_start(w_raw[:, i % 2], wffn[i]).then_inc(w_in[i % 2], 16)

                def split_next(i, p, i_in, hi, lo):
                    pool.wait_ge(w_in[p], i_in)
                    if not isinstance(i, int):
                        pool.sem_inc(passed["pool"], 1)
                    split_weights(nc, pool, w_raw[:, p], hi, lo, wh_done, i, w_split)
                    pool.wait_ge(w_split, i)
                    if not isinstance(i, int):
                        pool.sem_inc(passed["pool"], 1)
                        pool.dma_start(w_raw[:, p], wffn[bass.ds(i + 2, 1)].rearrange("o p n -> p (o n)")).then_inc(w_in[p], 16)
                    elif i + 2 < NE:
                        pool.dma_start(w_raw[:, p], wffn[i + 2]).then_inc(w_in[p], 16)

                def routed(e, q, i, p, i_in):
                    g = pool.value_load(route["first"][0:1, bass.ds(e - 1, 1)], min_val=1, max_val=NTILE - 4)
                    pool.wait_ge(ffn.down_ps, g + 1)
                    pool.sem_inc(passed["pool"], 1)
                    split_next(i, p, i_in, w_hi[:, q], w_lo[:, q])
                    pool.sem_inc(w_ready, 1)

                split_next(1, 1, 16, w_hi[:, 1], w_lo[:, 1])
                pool.sem_inc(w_ready, 1)
                with pool.Fori(0, SHARED // 2) as j:
                    for q in range(2):
                        i = j * 4 + (2 + 2 * q)
                        routed(j * 2 + (2 + q), q, i, 0, j * 32 + 16 * (q + 1))
                        split_next(i + 1, 1, j * 32 + 16 * (q + 2), wsh_hi[:, bass.ds(j * 2 + q, 1)].rearrange("p o n -> p (o n)"),
                                   wsh_lo[:, bass.ds(j * 2 + q, 1)].rearrange("p o n -> p (o n)"))
                E0 = 2 + SHARED
                with pool.Fori(0, (E - E0) // 2 - 1) as j:
                    for q in range(2):
                        routed(j * 2 + (E0 + q), q, j * 2 + (E0 + SHARED + q), q, j * 16 + 16 * (1 + SHARED + q))
                for q in range(2):
                    routed(E - 2 + q, q, NE - 2 + q, q, 16 * (NE // 2 - 1 + q))

            @block.scalar
            def _(act):
                act.preload_act_table(ACT.Silu)

                def high_x(g):
                    act.wait_ge(xT_ps, g + 1)
                    act.sem_inc(passed["act"], 1)
                    nc.scalar.copy(x_hi[:, :, bass.ds((g % 2) * T, T)],
                                   psX[:, :].rearrange("p (k t) -> p k t", k=KC)).then_inc(xh_ready, 1)

                def result(g):
                    act.wait_ge(ffn.down_ps, g + 2)
                    act.wait_ge(stored, g * 16 + 16)
                    act.sem_inc(passed["act"], 1)
                    nc.scalar.copy(y[:, bass.ds(g % 2, 1), :].rearrange("p o n -> p (o n)"), psD[:, :]).then_inc(y_ready, 1)

                def tile(g, before=True):
                    r = g % 2
                    ffn.gate_rest(nc, act, g, r)
                    high_x(g + 1)
                    ffn.gate0(nc, act, g, r)
                    ffn.high_rest(nc, act, g, 0)
                    if before:
                        result(g - 1)
                    ffn.high0(nc, act, g, 0)

                high_x(0)

                def expert(e, p, first):
                    expert_tiles(act, e, lambda g: tile(g, not first), tile)

                over_experts(expert)(act)
                expert(E - 1, 1, False)
                tiles = act.value_load(route["first"][0:1, E:E + 1], min_val=1, max_val=NTILE - 4)
                result(tiles - 1)

            @block.vector
            def _(dve):
                n_own = [0]

                def link(ins):
                    ins.then_inc(own, 1)
                    n_own[0] += 1
                    dve.wait_ge(own, n_own[0])

                ffn.start_vector(nc)
                nc.vector.sem_inc(y_ready, 1)

                def copy_rows(g):
                    dve.wait_ge(landed, g * 16 + 16)
                    dve.wait_ge(xT_ps, g)
                    if not isinstance(g, int):
                        dve.sem_inc(passed["dve"], 1)
                    nc.vector.tensor_copy(rows[:, :, :], ring[:, bass.ds(g % RING, 1)].rearrange("p o s h -> p (o s) h")).then_inc(copied, 1)

                def low_x(g):
                    cols = bass.ds((g % 2) * T, T)
                    dve.wait_ge(xh_ready, g + 1)
                    nc.vector.tensor_tensor(x_lo[:, :, cols], psX[:, :].rearrange("p (k t) -> p k t", k=KC),
                                            f32(x_hi[:, :, cols]), ALU.subtract).then_inc(xs_ready, 1)

                def tile(g):
                    r = g % 2
                    ffn.hidden_rest(nc, dve, g, r)
                    low_x(g + 1)
                    copy_rows(g + 2)
                    ffn.low_rest(nc, dve, g, 0)
                    ffn.hidden0(nc, dve, g, r)
                    ffn.low0(nc, dve, g, 0)

                link(chosen_rows(nc, link, route, moved, there))
                dve.wait_ge(landed, 16)
                nc.vector.tensor_copy(rows[:, :, :], ring[:, 0]).then_inc(copied, 1)
                low_x(0)
                copy_rows(1)

                def expert(e, p, first):
                    expert_tiles(dve, e, tile, tile)

                over_experts(expert)(dve)
                expert(E - 1, 1, False)

            @block.tensor
            def _(pe):
                ffn.start_tensor(pe)
                def transpose(g):
                    pe.wait_ge(copied, g + 1)
                    for k in range(KC):
                        for s in range(S):
                            last = nc.tensor.transpose(psX[:, k * T + s * P:k * T + (s + 1) * P],
                                                       rows[:, s, k * P:(k + 1) * P], ident[:, :])
                    last.then_inc(xT_ps, 1)

                def up(g, p, down_before=None):
                    pe.wait_ge(xs_ready, g + 1)
                    cols = bass.ds((g % 2) * T, T)

                    def between(c):
                        if c == 1:
                            transpose(g + 1)
                        if c == 0 and down_before is not None:
                            down(g - 1, down_before)

                    ffn.up(nc, pe, g, g % 2, w_hi[:, p], w_lo[:, p], lambda k: x_hi[:, k, cols], lambda k: x_lo[:, k, cols],
                           between)

                def down(g, p):
                    pe.wait_ge(y_ready, g + 1)
                    ffn.down(nc, pe, g, 0, w_hi[:, p], w_lo[:, p], [psD[:, s * H:(s + 1) * H] for s in range(S)])

                transpose(0)

                def expert(e, p, first):
                    def first_tile(g):
                        pe.wait_ge(w_ready, e + 1)
                        up(g, p, None if first else 1 - p)

                    def next_tile(g):
                        up(g, p, p)

                    expert_tiles(pe, e, first_tile, next_tile)

                over_experts(expert)(pe)
                expert(E - 1, 1, False)
                tiles = pe.value_load(route["first"][0:1, E:E + 1], min_val=1, max_val=NTILE - 4)
                down(tiles - 1, 1)


def shared_and_finish(nc, sb, psum, sem, w_raw, wsh_hi, wsh_lo, x_v, yg, xT_hi, xT_lo, s_sb, route, out_v, NT, NU):
    with ExitStack() as ctx:
        gate, weight, row4 = route["gate"], route["weight"], route["row4"]
        row_u = sb("row_u", [P, 2, S * TOPK], I32, ctx)
        ye = sb("ye", [P, 2, S, TOPK, H], F32, ctx)
        rows = w_raw[:, :, :].rearrange("p e n -> p (e n)")
        xf, yo = (rows[:, i * 2 * S * H:(i + 1) * 2 * S * H].rearrange("p (d s h) -> p d s h", d=2, s=S) for i in range(2))
        f = sb("f", [P, S, H], F32, ctx)
        fg = sb("fg", [P, S, H], F32, ctx)
        ffn = Ffn("s_", sb, psum, sem, ctx, 2)
        psD = [psum(f"s_psD{s}", ctx) for s in range(S)]

        x_in = [sem(f"s_x_in{i}", ctx) for i in range(2)]
        y_out = [sem(f"s_y_out{i}", ctx) for i in range(2)]
        ye_in = [sem(f"s_ye_in{i}", ctx) for i in range(2)]
        rows_set = sem("s_rows_set", ctx)
        taken = sem("s_taken", ctx)
        f_ready = sem("s_f_ready", ctx)
        fg_ready = sem("s_fg_ready", ctx)
        yo_ready = sem("s_yo_ready", ctx)
        own = sem("s_dve_own", ctx)
        passed = {k: sem(f"s_passed_{k}", ctx) for k in ("dve", "act", "pool")}
        GATHER = 16 * S * TOPK

        with nc.Block() as block:

            @block.sync
            def _(sp):
                for p in range(2):
                    sp.sem_inc(y_out[p], 16)
                    sp.dma_start(xf[:, p], x_v[p]).then_inc(x_in[p], 16)
                with sp.Fori(0, NU // 2) as n2:
                    for p in range(2):
                        n = n2 * 2 + p
                        sp.wait_ge(yo_ready, n + 3)
                        sp.dma_start(out_v[bass.ds(n, 1)].rearrange("o p s h -> p (o s) h"), yo[:, p]).then_inc(y_out[p], 16)
                        sp.dma_start(xf[:, p], x_v[bass.ds(n + 2, 1)].rearrange("o p s h -> p (o s) h")).then_inc(x_in[p], 16)
                for p in range(2):
                    sp.wait_ge(y_out[p], 16 * (NU // 2) + 16)
                    sp.wait_ge(x_in[p], 16 * (NU // 2 + 1))

            @block.gpsimd
            def _(pool):
                with pool.Fori(0, NU // 2) as n2:
                    for p in range(2):
                        n = n2 * 2 + p
                        pool.wait_ge(f_ready, n + 1)
                        pool.sem_inc(passed["pool"], 1)
                        nc.gpsimd.tensor_copy(row_u[:, p].rearrange("p (s k) -> p s k", s=S),
                                              row4[:, bass.ds(n * S, S), :]).then_inc(rows_set, 1)
                        pool.wait_ge(rows_set, n + 1)
                        pool.sem_inc(passed["pool"], 1)
                        for s in range(S):
                            for k in range(TOPK):
                                i = s * TOPK + k
                                nc.gpsimd.indirect_dma_start(
                                    ye[:, p, s, k, :], None, yg,
                                    bass.IndirectOffsetOnAxis(ap=row_u[:, p, i:i + 1].bitcast(mybir.dt.uint32), axis=0)
                                ).then_inc(ye_in[p], 16)

            @block.scalar
            def _(act):
                act.preload_act_table(ACT.Silu)

                def gated(n):
                    act.wait_ge(f_ready, n + 3)
                    act.wait_ge(yo_ready, n + 2)
                    act.sem_inc(passed["act"], 1)
                    nc.scalar.activation(fg[:, :, :], f[:, :, :], ACT.Silu).then_inc(fg_ready, 1)

                def take(m):
                    act.wait_ge(ffn.down_ps, m * SHARED + SHARED + 2)
                    act.wait_ge(fg_ready, m + 1)
                    act.wait_ge(f_ready, m + 2)
                    act.sem_inc(passed["act"], 1)
                    for s in range(S):
                        nc.scalar.activation(f[:, s, :], psD[s][:, 0:H], ACT.Copy,
                                             scale=gate[:, bass.ds(m * S + s, 1)]).then_inc(taken, 1)

                def unit(n, behind):
                    for j in range(SHARED):
                        q = n * SHARED + j
                        ffn.gate_rest(nc, act, q, j % 2)
                        if behind == 2 and j == 0:
                            gated(n - 2)
                        ffn.high_rest(nc, act, q, j % 2)
                        ffn.gate0(nc, act, q, j % 2)
                        ffn.high0(nc, act, q, j % 2)
                        if behind and j == 0:
                            take(n - 1)

                unit(0, 0)
                unit(1, 1)
                with act.Fori(2, NU) as n:
                    unit(n, 2)
                gated(NU - 2)
                take(NU - 1)
                gated(NU - 1)

            @block.vector
            def _(dve):
                ffn.start_vector(nc)
                nc.vector.sem_inc(taken, 2)
                nc.vector.sem_inc(fg_ready, 1)
                nc.vector.sem_inc(f_ready, 2)
                nc.vector.sem_inc(yo_ready, 2)
                PER_UNIT = S * TOPK

                def scalar_of(ap, t):
                    return ap[:, bass.ds(t, 1)]

                def step(n, j, before=None, middle=None, end=None):
                    q, r = n * SHARED + j, j % 2
                    if before:
                        before()
                    ffn.hidden_rest(nc, dve, q, r)
                    if middle:
                        middle()
                    ffn.low_rest(nc, dve, q, r)
                    ffn.hidden0(nc, dve, q, r)
                    if end:
                        end()
                    ffn.low0(nc, dve, q, r)

                def add(m, p, m_in, i):
                    k, s = divmod(i, S)
                    if k == 0:
                        dve.wait_ge(ye_in[p], m_in)
                        dve.wait_ge(taken, m * S + s + 3)
                    else:
                        dve.wait_ge(own, m * PER_UNIT + (i - S + 1))
                    nc.vector.scalar_tensor_tensor(out=f[:, s, :], in0=ye[:, p, s, k, :],
                                                   scalar=scalar_of(weight[:, k, :], m * S + s),
                                                   in1=f[:, s, :], op0=ALU.mult, op1=ALU.add).then_inc(own, 1)

                def sum_ready(m):
                    dve.wait_ge(own, m * PER_UNIT + PER_UNIT)
                    dve.sem_inc(f_ready, 1)

                def product(m):
                    dve.wait_ge(fg_ready, m + 2)
                    nc.vector.tensor_tensor(fg[:, :, :], fg[:, :, :], s_sb[:, bass.ds(m * S, S), :], ALU.mult).then_inc(passed["dve"], 1)

                def result(m, p, m_in):
                    dve.wait_ge(passed["dve"], m + 1)
                    dve.wait_ge(x_in[p], m_in)
                    dve.wait_ge(y_out[p], m_in)
                    nc.vector.tensor_tensor(yo[:, p], fg[:, :, :], xf[:, p], ALU.add).then_inc(yo_ready, 1)

                def unit(n, i, p):
                    if isinstance(n, int) and n < 2:
                        step(n, 0)
                    else:
                        step(n, 0, middle=lambda: product(n - 2), end=lambda: result(n - 2, p, i * 16))
                    if isinstance(n, int) and n < 1:
                        for j in range(1, SHARED):
                            step(n, j)
                        return
                    m, o = n - 1, 1 - p
                    m_in = i * GATHER + p * GATHER
                    step(n, 1, *[lambda a=a: add(m, o, m_in, a) for a in (0, 1, 2)])
                    step(n, 2, *[lambda a=a: add(m, o, m_in, a) for a in (3, 4, 5)])
                    step(n, 3, *[lambda a=a: add(m, o, m_in, a) for a in (6, 7)])
                    sum_ready(m)

                unit(0, 0, 0)
                unit(1, 0, 1)
                with dve.Fori(1, NU // 2) as i:
                    for p in range(2):
                        unit(i * 2 + p, i, p)
                m = NU - 1
                product(m - 1)
                result(m - 1, 0, (NU // 2) * 16)
                for a in range(PER_UNIT):
                    add(m, 1, (NU // 2) * GATHER, a)
                sum_ready(m)
                product(m)
                result(m, 1, (NU // 2) * 16)

            @block.tensor
            def _(pe):
                ffn.start_tensor(pe)

                def up(n, j):
                    cols = bass.ds(n * T, T)
                    ffn.up(nc, pe, n * SHARED + j, j % 2, wsh_hi[:, j], wsh_lo[:, j],
                           lambda k: xT_hi[:, k, cols], lambda k: xT_lo[:, k, cols])

                def down(n, j):
                    if j == 0:
                        pe.wait_ge(taken, n * S + 2)
                    ffn.down(nc, pe, n * SHARED + j, j % 2, wsh_hi[:, j], wsh_lo[:, j],
                             [psD[s][:, 0:H] for s in range(S)], first=j == 0, last_of_sum=j == SHARED - 1)

                up(0, 0)
                with pe.Fori(0, NU - 1) as n:
                    for j in range(1, SHARED):
                        up(n, j)
                        down(n, j - 1)
                    up(n + 1, 0)
                    down(n, SHARED - 1)
                for j in range(1, SHARED):
                    up(NU - 1, j)
                    down(NU - 1, j - 1)
                down(NU - 1, SHARED - 1)


def kernel(**inputs):
    import numpy as np
    import concourse.bacc as bacc
    from concourse.bass_utils import run_bass_kernel_spmd

    a = {k: np.asarray(v) for k, v in inputs.items()}
    x = a["L0_attn_x"]
    B, L, _ = x.shape
    f = x.dtype

    def zeros(*shape):
        return np.zeros(shape, f)

    def by_chunk(w):
        return np.ascontiguousarray(w.reshape(KC, P, -1).transpose(1, 0, 2).reshape(P, -1))

    wproj = by_chunk(np.concatenate([a["L0_attn_Wk"], a["L0_attn_Wv"], a["L0_attn_Wu"], a["L0_ffn_sgate_w"].T,
                                     a["L0_ffn_gate_w"].T, zeros(H, 1), a["L0_attn_Wq"]], 1))
    wo = by_chunk(a["L0_attn_Wo"])
    sgu = a["L0_ffn_shared_gate_up_w"].reshape(2, SHARED, I, H).transpose(1, 0, 2, 3)
    gu = np.concatenate([a["L0_ffn_w13"].reshape(E, 2, I, H), sgu], 0)
    dn = np.concatenate([a["L0_ffn_w2"], a["L0_ffn_shared_down_w"].reshape(H, SHARED, I).transpose(1, 0, 2)], 0)
    guT = gu.transpose(0, 3, 1, 2)
    pad = zeros(NE, H, P // 2 - IR)
    up = np.concatenate([guT[:, :, 0, :P], guT[:, :, 0, P:], pad, guT[:, :, 1, P:], pad, guT[:, :, 1, :P]], 2)
    up = up.reshape(NE, KC, P, NUP).transpose(0, 2, 1, 3).reshape(NE, P, CD)
    dT = dn.transpose(0, 2, 1)
    rest = np.concatenate([dT[:, P:], zeros(NE, P // 2 - IR, H)], 1)
    wffn = np.concatenate([up, dT[:, :P], np.concatenate([rest, rest], 1)], 2)
    order = [0, 1] + [i for j in range(SHARED) for i in (2 + j, E + j)] + list(range(2 + SHARED, E))
    wffn = np.ascontiguousarray(wffn[order])
    head = np.arange(P) // HEAD
    NTOK = B * L
    consts = np.concatenate([
        np.eye(P), (head[:, None] == head[None, :]) / float(HEAD), np.triu(np.ones((P, P)), 1),
        np.tile(1.0 + np.arange(E) * (NTOK + T), (P, 1)),
        np.tile(np.arange(NTILE) * float(T), (P, 1))], 1).astype(np.float32)
    xp = np.concatenate([x.reshape(B * L, H), zeros(2 * T, H)], 0)

    nc = bacc.Bacc("TRN2", target_bir_lowering=False, num_devices=1)
    arrays = {"x": xp, "wproj": wproj, "wo": wo, "wffn": wffn, "consts": consts}
    args = [nc.dram_tensor(n, v.shape, mybir.dt.from_np(v.dtype), kind="ExternalInput").ap() for n, v in arrays.items()]
    out = nc.dram_tensor("out", (B * L, H), F32, kind="ExternalOutput").ap()
    build(nc, *args, out)
    r = run_bass_kernel_spmd(nc, [arrays], core_ids=[0])
    return r.results[0]["out"].reshape(B, L, H)
```
